# Optimizing a Trainium2 kernel written in Bass

```python
import numpy as np
import jax
import jax.numpy as jnp

def _softmax(x, axis=-1):
    return jax.nn.softmax(x, axis=axis)

def _gelu(x):
    return jax.nn.gelu(x, approximate=True)

def _silu(x):
    return jax.nn.silu(x)

def _sigmoid(x):
    return jax.nn.sigmoid(x)

def _layernorm(x, axis=-1, eps=1e-05):
    m = jnp.mean(x, axis=axis, keepdims=True)
    v = jnp.var(x, axis=axis, keepdims=True)
    return (x - m) / jnp.sqrt(v + eps)

def _scatter_add(tgt, idx, src, axis=0):
    return tgt.at[idx].add(src)

def _segment_sum(src, seg, n):
    return jax.ops.segment_sum(src, seg, n)
kernel_name = 'mk_xattn_seq_d2_seqx_r4_d634e5'

def setup_inputs(seed: int=0):
    np.random.seed(seed)
    _w = jnp.asarray

    def _rec_inputs():
        import jax
        import jax.numpy as jnp
        _rk = jax.random.key(seed)
        x = 7.22e-05 + 1 * jax.random.normal(jax.random.fold_in(_rk, 1), (64, 128, 256), jnp.float32)
        _lenS = 128 - jax.random.randint(jax.random.fold_in(_rk, 7), (64,), 0, max(1, 128 // 4) + 1, jnp.int32)
        _lenS2 = 128 - jax.random.randint(jax.random.fold_in(_rk, 8), (64,), 0, max(1, 128 // 4) + 1, jnp.int32)
        _ctx_512P = jax.random.normal(jax.random.fold_in(_rk, 11), (64, 16, 128), jnp.float32)
        _ctx_512c = jax.random.dirichlet(jax.random.fold_in(_rk, 511), 0.3 * jnp.ones((16,), jnp.float32), (64, 128))
        _ctx_512t = jnp.einsum('bsk,bkd->bsd', _ctx_512c, _ctx_512P)
        _ctx_512t = _ctx_512t * jax.lax.rsqrt(jnp.mean(jnp.square(_ctx_512t)) + 1e-12) * 0.953939
        ctx_512 = 4.13588e-05 + 0.999923 * (_ctx_512t + 0.3 * jax.random.normal(jax.random.fold_in(_rk, 611), (64, 128, 128), jnp.float32))
        fside_BxSxS_0 = 0.000376506 + 0.999991 * jax.random.normal(jax.random.fold_in(_rk, 12), (64, 128, 128), jnp.float32)
        return (x, ctx_512, fside_BxSxS_0)
    x, ctx_512, fside_BxSxS_0 = _rec_inputs()

    def _L0_xattn_setup():
        import jax, jax.numpy as jnp
        import numpy as np
        EPS = 1e-05

        def _ln(x, g, b):
            mu = jnp.mean(x, axis=-1, keepdims=True)
            var = jnp.var(x, axis=-1, keepdims=True)
            return (x - mu) * jax.lax.rsqrt(var + EPS) * g + b

        def _cma(x1, x2, ln1_g, ln1_b, ln2_g, ln2_b, Wq, bq, Wk, bk, Wv, bv, Wo, bo):
            e = Wq.shape[1]
            scale = e ** (-0.5)
            x1n = _ln(x1, ln1_g, ln1_b)
            x2n = _ln(x2, ln2_g, ln2_b)
            q = x1n @ Wq + bq
            k = x2n @ Wk + bk
            v = x2n @ Wv + bv
            attn = jax.nn.softmax(jnp.einsum('bqe,bke->bqk', q, k) * scale, axis=-1)
            ctx = jnp.einsum('bqk,bke->bqe', attn, v)
            return ctx @ Wo + bo
        key = jax.random.key(seed)
        ks = jax.random.split(key, 24)
        B, Lt, La, Lv = (16, 128, 256, 128)
        Dt, Da, Dv, E = (256, 128, 128, 256)
        s = lambda k, *sh: jax.random.normal(k, sh, dtype=jnp.float32) * 0.02
        inp = {'text': jax.random.normal(ks[0], (B, Lt, Dt), dtype=jnp.float32), 'audio': jax.random.normal(ks[1], (B, La, Da), dtype=jnp.float32), 'video': jax.random.normal(ks[2], (B, Lv, Dv), dtype=jnp.float32), 'a_ln1_g': jnp.ones((Dt,)), 'a_ln1_b': jnp.zeros((Dt,)), 'a_ln2_g': jnp.ones((Da,)), 'a_ln2_b': jnp.zeros((Da,)), 'a_Wq': s(ks[3], Dt, E), 'a_bq': jnp.zeros((E,)), 'a_Wk': s(ks[4], Da, E), 'a_bk': jnp.zeros((E,)), 'a_Wv': s(ks[5], Da, E), 'a_bv': jnp.zeros((E,)), 'a_Wo': s(ks[6], E, Dt), 'a_bo': jnp.zeros((Dt,)), 'v_ln1_g': jnp.ones((Dt,)), 'v_ln1_b': jnp.zeros((Dt,)), 'v_ln2_g': jnp.ones((Dv,)), 'v_ln2_b': jnp.zeros((Dv,)), 'v_Wq': s(ks[7], Dt, E), 'v_bq': jnp.zeros((E,)), 'v_Wk': s(ks[8], Dv, E), 'v_bk': jnp.zeros((E,)), 'v_Wv': s(ks[9], Dv, E), 'v_bv': jnp.zeros((E,)), 'v_Wo': s(ks[10], E, Dt), 'v_bo': jnp.zeros((Dt,)), 'ln_g': jnp.ones((Dt,)), 'ln_b': jnp.zeros((Dt,)), 'fc_W': s(ks[11], Dt, Dt), 'fc_b': jnp.zeros((Dt,))}
        return inp
    _L0_xattn_all = _L0_xattn_setup()
    _L0_xattn_in = {k: v for k, v in _L0_xattn_all.items() if k in ('a_ln1_g', 'a_ln1_b', 'a_ln2_g', 'a_ln2_b', 'a_Wq', 'a_bq', 'a_Wk', 'a_bk', 'a_Wv', 'a_bv', 'a_Wo', 'a_bo', 'v_ln1_g', 'v_ln1_b', 'v_ln2_g', 'v_ln2_b', 'v_Wq', 'v_bq', 'v_Wk', 'v_bk', 'v_Wv', 'v_bv', 'v_Wo', 'v_bo', 'ln_g', 'ln_b', 'fc_W', 'fc_b')}
    del _L0_xattn_all

    def _L1_xattn_setup():
        import jax, jax.numpy as jnp
        import numpy as np
        QUERY_DIM = 256
        KEY_DIM = 128
        HIDDEN_DIM = 256
        B, LQ, LK = (8, 512, 512)
        key = jax.random.key(seed)
        ks = jax.random.split(key, 10)
        s_q = 1.0 / np.sqrt(QUERY_DIM)
        s_k = 1.0 / np.sqrt(KEY_DIM)
        s_h = 1.0 / np.sqrt(HIDDEN_DIM)
        return {'query': jax.random.normal(ks[0], (B, LQ, QUERY_DIM), jnp.float32), 'key': jax.random.normal(ks[1], (B, LK, KEY_DIM), jnp.float32), 'Wq': jax.random.uniform(ks[2], (QUERY_DIM, HIDDEN_DIM), jnp.float32, -s_q, s_q), 'bq': jax.random.uniform(ks[3], (HIDDEN_DIM,), jnp.float32, -s_q, s_q), 'Wk': jax.random.uniform(ks[4], (KEY_DIM, HIDDEN_DIM), jnp.float32, -s_k, s_k), 'bk': jax.random.uniform(ks[5], (HIDDEN_DIM,), jnp.float32, -s_k, s_k), 'Wv': jax.random.uniform(ks[6], (KEY_DIM, HIDDEN_DIM), jnp.float32, -s_k, s_k), 'bv': jax.random.uniform(ks[7], (HIDDEN_DIM,), jnp.float32, -s_k, s_k), 'Wo': jax.random.uniform(ks[8], (HIDDEN_DIM, QUERY_DIM), jnp.float32, -s_h, s_h), 'bo': jax.random.uniform(ks[9], (QUERY_DIM,), jnp.float32, -s_h, s_h)}
    _L1_xattn_all = _L1_xattn_setup()
    _L1_xattn_in = {k: v for k, v in _L1_xattn_all.items() if k in ('Wq', 'bq', 'Wk', 'bk', 'Wv', 'bv', 'Wo', 'bo')}
    del _L1_xattn_all
    return {'x': x, 'ctx_512': ctx_512, 'fside_BxSxS_0': fside_BxSxS_0, 'L0_xattn_a_ln1_g': _L0_xattn_in['a_ln1_g'], 'L0_xattn_a_ln1_b': _L0_xattn_in['a_ln1_b'], 'L0_xattn_a_ln2_g': _L0_xattn_in['a_ln2_g'], 'L0_xattn_a_ln2_b': _L0_xattn_in['a_ln2_b'], 'L0_xattn_a_Wq': _L0_xattn_in['a_Wq'], 'L0_xattn_a_bq': _L0_xattn_in['a_bq'], 'L0_xattn_a_Wk': _L0_xattn_in['a_Wk'], 'L0_xattn_a_bk': _L0_xattn_in['a_bk'], 'L0_xattn_a_Wv': _L0_xattn_in['a_Wv'], 'L0_xattn_a_bv': _L0_xattn_in['a_bv'], 'L0_xattn_a_Wo': _L0_xattn_in['a_Wo'], 'L0_xattn_a_bo': _L0_xattn_in['a_bo'], 'L0_xattn_v_ln1_g': _L0_xattn_in['v_ln1_g'], 'L0_xattn_v_ln1_b': _L0_xattn_in['v_ln1_b'], 'L0_xattn_v_ln2_g': _L0_xattn_in['v_ln2_g'], 'L0_xattn_v_ln2_b': _L0_xattn_in['v_ln2_b'], 'L0_xattn_v_Wq': _L0_xattn_in['v_Wq'], 'L0_xattn_v_bq': _L0_xattn_in['v_bq'], 'L0_xattn_v_Wk': _L0_xattn_in['v_Wk'], 'L0_xattn_v_bk': _L0_xattn_in['v_bk'], 'L0_xattn_v_Wv': _L0_xattn_in['v_Wv'], 'L0_xattn_v_bv': _L0_xattn_in['v_bv'], 'L0_xattn_v_Wo': _L0_xattn_in['v_Wo'], 'L0_xattn_v_bo': _L0_xattn_in['v_bo'], 'L0_xattn_ln_g': _L0_xattn_in['ln_g'], 'L0_xattn_ln_b': _L0_xattn_in['ln_b'], 'L0_xattn_fc_W': _L0_xattn_in['fc_W'], 'L0_xattn_fc_b': _L0_xattn_in['fc_b'], 'L1_xattn_Wq': _L1_xattn_in['Wq'], 'L1_xattn_bq': _L1_xattn_in['bq'], 'L1_xattn_Wk': _L1_xattn_in['Wk'], 'L1_xattn_bk': _L1_xattn_in['bk'], 'L1_xattn_Wv': _L1_xattn_in['Wv'], 'L1_xattn_bv': _L1_xattn_in['bv'], 'L1_xattn_Wo': _L1_xattn_in['Wo'], 'L1_xattn_bo': _L1_xattn_in['bo']}

def reference(x, ctx_512, fside_BxSxS_0, L0_xattn_a_ln1_g, L0_xattn_a_ln1_b, L0_xattn_a_ln2_g, L0_xattn_a_ln2_b, L0_xattn_a_Wq, L0_xattn_a_bq, L0_xattn_a_Wk, L0_xattn_a_bk, L0_xattn_a_Wv, L0_xattn_a_bv, L0_xattn_a_Wo, L0_xattn_a_bo, L0_xattn_v_ln1_g, L0_xattn_v_ln1_b, L0_xattn_v_ln2_g, L0_xattn_v_ln2_b, L0_xattn_v_Wq, L0_xattn_v_bq, L0_xattn_v_Wk, L0_xattn_v_bk, L0_xattn_v_Wv, L0_xattn_v_bv, L0_xattn_v_Wo, L0_xattn_v_bo, L0_xattn_ln_g, L0_xattn_ln_b, L0_xattn_fc_W, L0_xattn_fc_b, L1_xattn_Wq, L1_xattn_bq, L1_xattn_Wk, L1_xattn_bk, L1_xattn_Wv, L1_xattn_bv, L1_xattn_Wo, L1_xattn_bo):
    import jax
    import jax.numpy as jnp

    def _L0_xattn_ref(text, audio, video, a_ln1_g, a_ln1_b, a_ln2_g, a_ln2_b, a_Wq, a_bq, a_Wk, a_bk, a_Wv, a_bv, a_Wo, a_bo, v_ln1_g, v_ln1_b, v_ln2_g, v_ln2_b, v_Wq, v_bq, v_Wk, v_bk, v_Wv, v_bv, v_Wo, v_bo, ln_g, ln_b, fc_W, fc_b):
        import jax, jax.numpy as jnp
        import numpy as np
        EPS = 1e-05

        def _ln(x, g, b):
            mu = jnp.mean(x, axis=-1, keepdims=True)
            var = jnp.var(x, axis=-1, keepdims=True)
            return (x - mu) * jax.lax.rsqrt(var + EPS) * g + b

        def _cma(x1, x2, ln1_g, ln1_b, ln2_g, ln2_b, Wq, bq, Wk, bk, Wv, bv, Wo, bo):
            e = Wq.shape[1]
            scale = e ** (-0.5)
            x1n = _ln(x1, ln1_g, ln1_b)
            x2n = _ln(x2, ln2_g, ln2_b)
            q = x1n @ Wq + bq
            k = x2n @ Wk + bk
            v = x2n @ Wv + bv
            attn = jax.nn.softmax(jnp.einsum('bqe,bke->bqk', q, k) * scale, axis=-1)
            ctx = jnp.einsum('bqk,bke->bqe', attn, v)
            return ctx @ Wo + bo
        out_a = _cma(text, audio, a_ln1_g, a_ln1_b, a_ln2_g, a_ln2_b, a_Wq, a_bq, a_Wk, a_bk, a_Wv, a_bv, a_Wo, a_bo)
        out_v = _cma(text, video, v_ln1_g, v_ln1_b, v_ln2_g, v_ln2_b, v_Wq, v_bq, v_Wk, v_bk, v_Wv, v_bv, v_Wo, v_bo)
        output = out_a + out_v + text
        residual = output
        output = _ln(output, ln_g, ln_b) @ fc_W + fc_b
        return output + residual

    def _L1_xattn_ref(query, key, Wq, bq, Wk, bk, Wv, bv, Wo, bo):
        import jax, jax.numpy as jnp
        import numpy as np
        QUERY_DIM = 256
        KEY_DIM = 128
        HIDDEN_DIM = 256
        B, LQ, LK = (8, 512, 512)
        scale = HIDDEN_DIM ** (-0.5)
        Q = jnp.einsum('bqd,dh->bqh', query, Wq) + bq
        K = jnp.einsum('bkd,dh->bkh', key, Wk) + bk
        V = jnp.einsum('bkd,dh->bkh', key, Wv) + bv
        scores = jnp.einsum('bqh,bkh->bqk', Q, K) * scale
        weights = jax.nn.softmax(scores, axis=-1)
        attended = jnp.einsum('bqk,bkh->bqh', weights, V)
        out = jnp.einsum('bqh,hd->bqd', attended, Wo) + bo
        return query + out
    x = _L0_xattn_ref(x, ctx_512, fside_BxSxS_0, L0_xattn_a_ln1_g, L0_xattn_a_ln1_b, L0_xattn_a_ln2_g, L0_xattn_a_ln2_b, L0_xattn_a_Wq, L0_xattn_a_bq, L0_xattn_a_Wk, L0_xattn_a_bk, L0_xattn_a_Wv, L0_xattn_a_bv, L0_xattn_a_Wo, L0_xattn_a_bo, L0_xattn_v_ln1_g, L0_xattn_v_ln1_b, L0_xattn_v_ln2_g, L0_xattn_v_ln2_b, L0_xattn_v_Wq, L0_xattn_v_bq, L0_xattn_v_Wk, L0_xattn_v_bk, L0_xattn_v_Wv, L0_xattn_v_bv, L0_xattn_v_Wo, L0_xattn_v_bo, L0_xattn_ln_g, L0_xattn_ln_b, L0_xattn_fc_W, L0_xattn_fc_b)
    x = _L1_xattn_ref(x, ctx_512, L1_xattn_Wq, L1_xattn_bq, L1_xattn_Wk, L1_xattn_bk, L1_xattn_Wv, L1_xattn_bv, L1_xattn_Wo, L1_xattn_bo)
    return x

_drawn_inputs = setup_inputs


def setup_inputs(seed=0):
    import zlib

    import numpy as np

    out = dict(_drawn_inputs(seed))
    spreads = {'L0_xattn_a_ln1_g': (1.0, 0.6),
     'L0_xattn_a_ln1_b': (0.0, 0.8),
     'L0_xattn_a_ln2_g': (1.0, 0.6),
     'L0_xattn_a_ln2_b': (0.0, 0.8),
     'L0_xattn_a_bq': (0.0, 2.0),
     'L0_xattn_a_bk': (0.0, 2.0),
     'L0_xattn_a_bv': (0.0, 0.295),
     'L0_xattn_a_bo': (0.0, 0.1),
     'L0_xattn_v_ln1_g': (1.0, 0.6),
     'L0_xattn_v_ln1_b': (0.0, 0.8),
     'L0_xattn_v_ln2_g': (1.0, 0.6),
     'L0_xattn_v_ln2_b': (0.0, 0.8),
     'L0_xattn_v_bq': (0.0, 0.8),
     'L0_xattn_v_bk': (0.0, 2.0),
     'L0_xattn_v_bv': (0.0, 0.3),
     'L0_xattn_v_bo': (0.0, 0.1),
     'L0_xattn_ln_g': (1.0, 0.2),
     'L0_xattn_ln_b': (0.0, 0.307),
     'L0_xattn_fc_b': (0.0, 0.1)}
    factors = {'fside_BxSxS_0': 8.0,
     'L0_xattn_a_Wq': 8.0,
     'L0_xattn_a_Wk': 8.0,
     'L0_xattn_v_Wq': 8.0,
     'L0_xattn_v_Wk': 8.0,
     'L0_xattn_v_Wv': 6.318,
     'L1_xattn_bq': 56.788,
     'L1_xattn_bk': 64.0}
    for name, (base, spread) in spreads.items():
        noise = np.random.default_rng([zlib.crc32(name.encode()), seed]).standard_normal(out[name].shape)
        drawn = base * np.exp(spread * noise) if base else spread * noise
        out[name] = jnp.asarray(drawn.astype(out[name].dtype))
    for name, factor in factors.items():
        out[name] = (out[name] * factor).astype(out[name].dtype)
    return out
```

```python
import concourse.bass as bass
from concourse import mybir
from contextlib import ExitStack

F32 = mybir.dt.float32
F32R = mybir.dt.float32r
ALU = mybir.AluOpType
ACT = mybir.ActivationFunctionType
AX = mybir.AxisListType

BATCH, SEQ, DQ, DK, E = 64, 128, 256, 128, 256
EPS = 1e-5
SCALE = float(E) ** -0.5
PER = 2
NG = BATCH // PER
CQ, CE = DQ // 128, E // 128
UNROLL = 4
FIRST = 6
LOOPS = (NG - 2 - FIRST) // UNROLL
LAST = NG + 2

ADD = 0
G1, B1 = 14, 18
G2, B2 = 22, 24
LNG, LNB = 26, 28
BQ1, BK1, BV1 = 30, 32, 34
NCOL = 36


def build(nc, x, ctx, fside, w, cols, rows, g2rows, out):
    with ExitStack() as stack:
        def sb(name, shape, dt=F32):
            return stack.enter_context(nc.sbuf_tensor(name, shape, dt))

        def sem(name):
            return stack.enter_context(nc.semaphore(name))

        Wq = [sb(f"Wq{a}", [128, CQ, E]) for a in range(3)]
        WqT = [sb(f"WqT{a}", [128, CE, DQ]) for a in range(3)]
        Wk = [sb(f"Wk{a}", [128, E]) for a in range(2)]
        WkT = [sb(f"WkT{a}", [128, CE, DK]) for a in range(3)]
        Wv = [sb(f"Wv{a}", [128, E]) for a in range(2)]
        WvT = [sb(f"WvT{a}", [128, CE, DK]) for a in range(3)]
        Wo = [sb(f"Wo{a}", [128, CE, DQ]) for a in range(3)]
        fcW = sb("fcW", [128, CQ, DQ])
        col = sb("col", [128, NCOL])
        row = sb("row", [1, 4, DQ])
        g2b = sb("g2b", [128, 2, DK])

        zeros = sb("zeros", [128, 128])
        ident = sb("ident", [128, 128])
        center = sb("center", [128, 128])
        neg = sb("neg", [128, 128])
        ones = sb("ones", [1, 128])
        nhalf = sb("nhalf", [128, 6])
        invn = sb("invn", [128, 6])
        shift = sb("shift", [128, 6])

        vec = sb("vec", [128, 14])
        g1s = sb("g1s", [128, 4])
        U = sb("U", [128, 4, DK])
        Urow = sb("Urow", [1, 2, DK])
        usum = sb("usum", [128, 6])
        usc = sb("usc", [128, 6])
        crow = sb("crow", [1, 2, DK])
        Wg = sb("Wg", [128, 2, DQ])
        brow = sb("brow", [1, 2, DQ])
        Fg = sb("Fg", [128, CQ, DQ])
        frow = sb("frow", [1, 2, DQ])
        qb1 = sb("qb1", [128, 2])
        bkrep = sb("bkrep", [128, CE, 128])
        Af = sb("Af", [128, CQ, 2, DK])
        Ahi, Alo = sb("Ahi", [128, CQ, 2, DK], F32R), sb("Alo", [128, CQ, 2, DK], F32R)
        Whi, Wlo = sb("Whi", [128, 3, DQ], F32R), sb("Wlo", [128, 3, DQ], F32R)
        Fhi, Flo = sb("Fhi", [128, CQ, DQ], F32R), sb("Flo", [128, CQ, DQ], F32R)
        M1 = sb("M1", [128, CQ, DK])
        wr1 = sb("wr1", [128, DQ])
        cc = sb("cc", [128, 4])

        X = [sb(f"X{k}", [128, PER, DQ]) for k in range(4)]
        YV = [sb(f"YV{k}", [128, 2, PER, DK]) for k in range(2)]
        Y1 = [sb(f"Y1{k}", [128, PER, DK]) for k in range(4)]
        inst = [sb(f"inst{k}", [128, 6, 6]) for k in range(2)]
        outst = [sb(f"outst{k}", [128, PER, 6]) for k in range(2)]
        inw = sb("inw", [128, 10, 6])
        outw = sb("outw", [128, 10, PER])
        xn = [sb(f"xn{k}", [128, PER, DQ]) for k in range(2)]
        yvn = [sb(f"yvn{k}", [128, 2, PER, DK]) for k in range(4)]
        xhi, xlo = sb("xhi", [128, 512], F32R), sb("xlo", [128, 512], F32R)
        yvT = sb("yvT", [128, 512])
        tT = sb("tT", [128, 512])
        nmax = sb("nmax", [128, 4])
        rs = sb("rs", [128, 4])
        ri = sb("ri", [128, 4])
        prob = sb("prob", [128, 4, 128])
        probT = sb("probT", [128, 512])
        chi, clo = sb("chi", [128, 512], F32R), sb("clo", [128, 512], F32R)
        O = [sb(f"O{k}", [128, PER, DQ]) for k in range(2)]
        on = [sb(f"on{k}", [128, PER, DQ]) for k in range(2)]
        ohi, olo = sb("ohi", [128, 512], F32R), sb("olo", [128, 512], F32R)
        X1 = [sb(f"X1{k}", [128, PER, DQ]) for k in range(2)]
        junk = sb("junk", [128, PER, DQ])
        r1 = [sb(f"r1{k}", [128, PER]) for k in range(2)]
        x1T = sb("x1T", [128, 512])
        y1T = [sb(f"y1T{k}", [128, 256]) for k in range(2)]
        t1T = sb("t1T", [128, 256])
        max1, top1, nmax1 = sb("max1", [128, PER]), sb("top1", [128, PER]), sb("nmax1", [128, PER])
        rs1, ri1 = sb("rs1", [128, PER]), sb("ri1", [128, PER])
        prob1 = sb("prob1", [128, PER, 128])
        prob1T = sb("prob1T", [128, 256])
        c1hi, c1lo = sb("c1hi", [128, 256], F32R), sb("c1lo", [128, 256], F32R)
        fin = [sb(f"fin{k}", [128, PER, DQ]) for k in range(2)]

        bank = [stack.enter_context(nc.psum_tensor(f"bank{k}", [128, 512], F32)) for k in range(8)]

        w_loaded = sem("w_loaded")
        consts_made = sem("consts_made")
        idents_made = sem("idents_made")
        vecs_multiplied = sem("vecs_multiplied")
        vecs_added = sem("vecs_added")
        weights_multiplied = sem("weights_multiplied")
        weights_scaled = sem("weights_scaled")
        weights_step = sem("weights_step")
        weights_centred = sem("weights_centred")
        weights_ready = sem("weights_ready")
        x_loaded = [sem(f"x_loaded{k}") for k in range(4)]
        yv_loaded = [sem(f"yv_loaded{k}") for k in range(2)]
        y1_loaded = [sem(f"y1_loaded{k}") for k in range(4)]
        stored = [sem(f"stored{k}") for k in range(2)]
        in_stats = sem("in_stats")
        in_step = sem("in_step")
        in_normed = sem("in_normed")
        scalars_awaited = sem("scalars_awaited")
        xT_ready, yvT_ready = sem("xT_ready"), sem("yvT_ready")
        xhi_made, x_split, yvT_copied = sem("xhi_made"), sem("x_split"), sem("yvT_copied")
        t_ready, tT_copied = sem("t_ready"), sem("tT_copied")
        s_ready, max_found, exp_done = sem("s_ready"), sem("max_found"), sem("exp_done")
        sum_inverted, prob_normed = sem("sum_inverted"), sem("prob_normed")
        probT_ready, probT_copied = sem("probT_ready"), sem("probT_copied")
        ctxT_ready, chi_made, c_split = sem("ctxT_ready"), sem("chi_made"), sem("c_split")
        proj_ready, o_added = sem("proj_ready"), sem("o_added")
        out_stats, out_step, o_normed = sem("out_stats"), sem("out_step"), sem("o_normed")
        oT_ready, ohi_made, o_split = sem("oT_ready"), sem("ohi_made"), sem("o_split")
        fc_ready, x1_added, r1_found = sem("fc_ready"), sem("x1_added"), sem("r1_found")
        x1T_ready, x1T_copied, y1T_copied = sem("x1T_ready"), sem("x1T_copied"), sem("y1T_copied")
        t1_ready, t1T_copied = sem("t1_ready"), sem("t1T_copied")
        s1_ready, max1_found, top1_found, nmax1_found = sem("s1_ready"), sem("max1_found"), sem("top1_found"), sem("nmax1_found")
        exp1_done, sum1_inverted, prob1_normed = sem("exp1_done"), sem("sum1_inverted"), sem("prob1_normed")
        prob1T_ready, prob1T_copied = sem("prob1T_ready"), sem("prob1T_copied")
        ctx1T_ready, c1hi_made, c1_split = sem("ctx1T_ready"), sem("c1hi_made"), sem("c1_split")
        proj1_ready, final_added = sem("proj1_ready"), sem("final_added")

        block = stack.enter_context(nc.Block())

        x_g = x.rearrange("(g b) q d -> g q b d", b=PER)
        ctx_g = ctx.rearrange("(g b) q d -> g q b d", b=PER)
        fside_g = fside.rearrange("(g b) q d -> g q b d", b=PER)
        out_g = out.rearrange("(g b) q d -> g q b d", b=PER)

        def live(it, c):
            return not isinstance(it, int) or 0 <= UNROLL * it + c < NG

        def upto(it, c, k=1):
            return it * (UNROLL * k) + k * (c + 1)

        def nth(it, c, slots, k=16):
            return it * (k * UNROLL // slots) + k * (c // slots + 1)

        def wait(eng, s, value):
            if not isinstance(value, int) or value > 0:
                eng.wait_ge(s, value)

        def run(eng, iteration, start=-2):
            for c in range(start, FIRST):
                iteration(0, c)
            with eng.Fori(0, LOOPS) as it:
                for c in range(FIRST, FIRST + UNROLL):
                    iteration(it, c)
            for c in range(FIRST, LAST + 1 - UNROLL * LOOPS):
                iteration(LOOPS, c)

        @block.sync
        def _(sp):
            def iteration(it, c):
                g = it * UNROLL + c
                if live(it, c + 2):
                    n = c + 2
                    wait(sp, o_added, upto(it, n - 4))
                    sp.dma_start(X[n % 4][:], x_g[g + 2]).then_inc(x_loaded[n % 4], 16)
                    wait(sp, in_normed, upto(it, n - 2))
                    sp.dma_start(YV[n % 2][:, 0], ctx_g[g + 2]).then_inc(yv_loaded[n % 2], 16)
                    sp.dma_start(YV[n % 2][:, 1], fside_g[g + 2]).then_inc(yv_loaded[n % 2], 16)
                if live(it, c):
                    wait(sp, ctx1T_ready, upto(it, c - 4))
                    sp.dma_start(Y1[c % 4][:], ctx_g[g]).then_inc(y1_loaded[c % 4], 16)
                if live(it, c - 3):
                    sp.wait_ge(final_added, upto(it, c - 3))
                    sp.dma_start(out_g[g - 3], fin[(c - 3) % 2][:]).then_inc(stored[(c - 3) % 2], 16)

            run(sp, iteration)
            for k in range(2):
                sp.wait_ge(stored[k], 16 * NG // 2)

        @block.gpsimd
        def _(pool):
            pool.memset(zeros[:], 0.0).then_inc(consts_made, 1)
            pool.memset(neg[:], -1.0 / DQ).then_inc(consts_made, 1)
            pool.memset(center[:], -1.0 / DK).then_inc(consts_made, 1)
            pool.memset(ones[:], 1.0).then_inc(consts_made, 1)
            pool.memset(nhalf[:], -0.5).then_inc(consts_made, 1)
            pool.memset(invn[:, 0:PER], 1.0 / DQ).then_inc(consts_made, 1)
            pool.memset(invn[:, PER:6], 1.0 / DK).then_inc(consts_made, 1)
            pool.memset(shift[:, 0:PER], 0.0).then_inc(consts_made, 1)
            pool.memset(shift[:, PER:6], 1.0 / DK).then_inc(consts_made, 1)
            pool.wait_ge(consts_made, 9)
            pool.affine_select(out=ident[:], in_=zeros[:], compare_op=ALU.not_equal, fill=1.0, base=0,
                               pattern=[[-1, 128]], channel_multiplier=1).then_inc(idents_made, 1)
            pool.affine_select(out=center[:], in_=center[:], compare_op=ALU.not_equal, fill=1.0 - 1.0 / DK, base=0,
                               pattern=[[-1, 128]], channel_multiplier=1).then_inc(idents_made, 1)

            def before_scalars(value_ready, value):
                pool.wait_ge(value_ready, value)
                pool.sem_inc(scalars_awaited, 1)

            def rstd_and_shift(st, wk, n, done, base, inv, add):
                def step(k, ins):
                    ins.then_inc(done, 1)

                me, mo, se, so = st[:, :, 1], st[:, :, 4], st[:, :, 2], st[:, :, 5]
                step(1, pool.tensor_tensor(wk[:, 0, 0:n], me, mo, ALU.add))
                step(2, pool.tensor_tensor(wk[:, 1, 0:n], me, mo, ALU.subtract))
                step(3, pool.tensor_tensor(wk[:, 2, 0:n], se, so, ALU.add))
                pool.wait_ge(done, base(2))
                step(4, pool.tensor_tensor(wk[:, 3, 0:n], wk[:, 1, 0:n], wk[:, 1, 0:n], ALU.mult))
                pool.wait_ge(done, base(3))
                step(5, pool.tensor_tensor(wk[:, 4, 0:n], wk[:, 2, 0:n], inv, ALU.mult))
                before_scalars(done, base(4))
                step(6, pool.tensor_scalar(wk[:, 5, 0:n], wk[:, 3, 0:n], 0.25, EPS, ALU.mult, ALU.add))
                pool.wait_ge(done, base(6))
                step(7, pool.tensor_tensor(wk[:, 6, 0:n], wk[:, 4, 0:n], wk[:, 5, 0:n], ALU.add))
                step(8, pool.tensor_scalar(wk[:, 8, 0:n], wk[:, 0, 0:n], -0.5, 0.0, ALU.mult, ALU.add))
                pool.wait_ge(done, base(7))
                step(9, pool.tensor_tensor(wk[:, 7, 0:n], wk[:, 6, 0:n], nhalf[:, 0:n], ALU.pow))
                pool.wait_ge(done, base(9))
                step(10, pool.tensor_tensor(wk[:, 3, 0:n], wk[:, 8, 0:n], wk[:, 7, 0:n], ALU.mult))
                pool.wait_ge(done, base(10))
                step(11, pool.tensor_tensor(wk[:, 9, 0:n], wk[:, 3, 0:n], add, ALU.add))

            STEPS = 11

            def iteration(it, c):
                if live(it, c + 1):
                    n = c + 1
                    pool.wait_ge(in_stats, upto(it, n))
                    rstd_and_shift(inst[n % 2], inw, 6, in_step, lambda k: upto(it, n - 1, STEPS) + k, invn[:], shift[:])
                    wait(pool, xT_ready, upto(it, n - 2))
                    wait(pool, ctxT_ready, upto(it, n - 4))
                    before_scalars(in_step, upto(it, n, STEPS))
                    for b in range(PER):
                        pool.tensor_scalar(xn[n % 2][:, b, :], X[n % 4][:, b, :], inw[:, 7, b:b + 1], inw[:, 9, b:b + 1],
                                           ALU.mult, ALU.add)
                    for a in range(2):
                        for b in range(PER):
                            j = PER + PER * a + b
                            last = pool.tensor_scalar(yvn[n % 4][:, a, b, :], YV[n % 2][:, a, b, :], inw[:, 7, j:j + 1],
                                                      inw[:, 9, j:j + 1], ALU.mult, ALU.add)
                    last.then_inc(in_normed, 1)
                if live(it, c - 1):
                    n = c - 1
                    pool.wait_ge(out_stats, upto(it, n))
                    rstd_and_shift(outst[n % 2], outw, PER, out_step, lambda k: upto(it, n - 1, STEPS) + k,
                                   invn[:, 0:PER], neg_shift)
                    wait(pool, oT_ready, upto(it, n - 2))
                    before_scalars(out_step, upto(it, n, STEPS))
                    for b in range(PER):
                        last = pool.tensor_scalar(on[n % 2][:, b, :], O[n % 2][:, b, :], outw[:, 7, b:b + 1],
                                                  outw[:, 9, b:b + 1], ALU.mult, ALU.add)
                    last.then_inc(o_normed, 1)

            neg_shift = invn[:, 0:PER]
            run(pool, iteration)

        @block.scalar
        def _(act):
            n = 0
            for t, src in [(col, cols), (row, rows), (g2b, g2rows.partition_broadcast(128))]:
                act.dma_start(t[:], src).then_inc(w_loaded, 16)
                n += 1
            for a in range(3):
                for t, key in [(Wq, "Wq"), (Wk, "Wk"), (Wv, "Wv"), (Wo, "Wo"), (WqT, "WqT"), (WkT, "WkT"), (WvT, "WvT")]:
                    if a == 2 and key in ("Wk", "Wv"):
                        continue
                    src = w[f"{key}{a}"]
                    if key not in ("Wk", "Wv"):
                        src = src.rearrange("(c p) n -> p c n", p=128)
                    act.dma_start(t[a][:], src).then_inc(w_loaded, 16)
                    n += 1
            act.dma_start(fcW[:], w["fcW"].rearrange("(c p) n -> p c n", p=128)).then_inc(w_loaded, 16)
            assert n + 1 == NLOADS
            act.wait_ge(weights_ready, 1)

            def copy(dst, src, s):
                act.activation(dst, src, ACT.Copy).then_inc(s, 1)

            def iteration(it, c):
                if live(it, c):
                    act.wait_ge(xT_ready, upto(it, c))
                    copy(xhi[:], bank[0][:], xhi_made)
                if live(it, c - 3):
                    act.wait_ge(nmax1_found, upto(it, c - 3))
                    for b in range(PER):
                        last = act.activation(prob1[:, b, :], bank[2][:, 128 * b:128 * b + 128], ACT.Exp,
                                              bias=nmax1[:, b:b + 1], scale=1.0, accum_out=rs1[:, b:b + 1])
                    last.then_inc(exp1_done, 1)
                if live(it, c - 1):
                    act.wait_ge(probT_ready, upto(it, c - 1))
                    copy(probT[:], bank[3][:], probT_copied)
                if live(it, c - 2):
                    act.wait_ge(oT_ready, upto(it, c - 2))
                    copy(ohi[:], bank[4][:], ohi_made)
                if live(it, c - 1):
                    act.wait_ge(ctxT_ready, upto(it, c - 1))
                    copy(chi[:], bank[6][:], chi_made)
                if live(it, c - 3):
                    act.wait_ge(prob1T_ready, upto(it, c - 3))
                    copy(prob1T[:], bank[7][:, 0:256], prob1T_copied)
                if live(it, c):
                    act.wait_ge(yvT_ready, upto(it, c))
                    copy(yvT[:], bank[1][:], yvT_copied)
                    act.wait_ge(t_ready, upto(it, c))
                    for a in range(2):
                        last = act.activation(tT[:, 256 * a:256 * a + 256], bank[5][:, 256 * a:256 * a + 256],
                                              ACT.Identity, bias=cc[:, a:a + 1], scale=1.0)
                    last.then_inc(tT_copied, 1)
                if live(it, c - 3):
                    act.wait_ge(ctx1T_ready, upto(it, c - 3))
                    copy(c1hi[:], bank[1][:, 0:256], c1hi_made)
                if live(it, c - 2):
                    act.wait_ge(x1T_ready, upto(it, c - 2))
                    copy(x1T[:], bank[3][:], x1T_copied)
                    copy(y1T[(c - 2) % 2][:], bank[4][:, 0:256], y1T_copied)
                if live(it, c):
                    act.wait_ge(max_found, upto(it, c))
                    for j in range(4):
                        last = act.activation(prob[:, j, :], bank[5][:, 128 * j:128 * j + 128], ACT.Exp,
                                              bias=nmax[:, j:j + 1], scale=1.0, accum_out=rs[:, j:j + 1])
                    last.then_inc(exp_done, 1)
                if live(it, c - 2):
                    act.wait_ge(t1_ready, upto(it, c - 2))
                    act.activation(t1T[:], bank[6][:, 0:256], ACT.Identity, bias=cc[:, 2:3], scale=1.0).then_inc(t1T_copied, 1)

            run(act, iteration, start=0)

        @block.tensor
        def _(pe):
            def split(dst, hi, lo, rhi, rlo, first, last):
                pe.matmul(dst, hi, rhi, start=first, stop=False)
                pe.matmul(dst, hi, rlo, start=False, stop=False)
                return pe.matmul(dst, lo, rhi, start=False, stop=last)

            pe.wait_ge(w_loaded, 16 * NLOADS)
            v = bank[0]
            for a in range(2):
                for e in range(CE):
                    es = slice(128 * e, 128 * e + 128)
                    at = 6 * a + e
                    pe.matmul(v[:, at:at + 1], Wk[a][:, es], col[:, B2 + a:B2 + a + 1], start=True, stop=True)
                    for d in range(CQ):
                        pe.matmul(v[:, at + 2:at + 3], Wq[a][:, d, es], col[:, B1 + 2 * a + d:B1 + 2 * a + d + 1],
                                  start=(d == 0), stop=(d == CQ - 1))
                    pe.matmul(v[:, at + 4:at + 5], Wv[a][:, es], col[:, B2 + a:B2 + a + 1], start=True, stop=True)
            for d in range(CQ):
                for e in range(CE):
                    last = pe.matmul(v[:, 12 + d:13 + d], Wo[2][:, e, 128 * d:128 * d + 128], col[:, BV1 + e:BV1 + e + 1],
                                     start=(e == 0), stop=(e == CE - 1))
            last.then_inc(vecs_multiplied, 1)
            pe.wait_ge(vecs_added, 1)

            def times_keys(dst, at, lhsT, a):
                for e in range(CE):
                    pe.matmul(dst[:, at:at + 128], lhsT(e), WkT[a][:, e, :], start=(e == 0), stop=(e == CE - 1))
                for e in range(CE):
                    pe.matmul(dst[:, at + 128:at + 129], lhsT(e), vec[:, 6 * a + e:6 * a + e + 1],
                              start=(e == 0), stop=(e == CE - 1))

            for a in range(2):
                for d in range(CQ):
                    times_keys(bank[1 + a], 192 * d, lambda e: WqT[a][:, e, 128 * d:128 * d + 128], a)
                times_keys(bank[3][0:1], 192 * a, lambda e: vec[:, 6 * a + 2 + e:6 * a + 3 + e], a)
                for e in range(CE):
                    pe.matmul(bank[4][:, 256 * a:256 * a + 256], WvT[a][:, e, :], Wo[a][:, e, :],
                              start=(e == 0), stop=(e == CE - 1))
                for e in range(CE):
                    pe.matmul(bank[6][0:1, 256 * a:256 * a + 256], vec[:, 6 * a + 4 + e:6 * a + 5 + e], Wo[a][:, e, :],
                              start=(e == 0), stop=(e == CE - 1))
            for e in range(CE):
                for d in range(CQ):
                    pe.matmul(bank[7][:, e:e + 1], Wq[2][:, d, 128 * e:128 * e + 128], vec[:, 12 + d:13 + d],
                              start=(d == 0), stop=(d == CQ - 1))
            for e in range(CE):
                pe.matmul(bank[7][0:1, 256:512], col[:, BV1 + e:BV1 + e + 1], Wo[2][:, e, :], start=(e == 0), stop=False)
            for d in range(CQ):
                last = pe.matmul(bank[7][0:1, 256:512], col[:, LNB + d:LNB + d + 1], fcW[:, d, :],
                                 start=False, stop=(d == CQ - 1))
            last.then_inc(weights_multiplied, 1)
            pe.wait_ge(weights_scaled, 1)
            pe.wait_ge(idents_made, 2)
            for a in range(2):
                pe.matmul(bank[0][:, a:a + 1], crow[0:1, a, :], ones[0:1, 0:1], start=True, stop=True)
            for e in range(CE):
                pe.matmul(bank[0][:, 2:3], WkT[2][:, e, :], qb1[:, e:e + 1], start=(e == 0), stop=(e == CE - 1))
            for e in range(CE):
                pe.matmul(bank[0][:, 3:4], bkrep[:, e, :], qb1[:, e:e + 1], start=(e == 0), stop=(e == CE - 1))
            for a in range(2):
                dst = bank[1][:, 256 * a:256 * a + 256]
                pe.matmul(dst, center[:], Wg[:, a, :], start=True, stop=False)
                pe.matmul(dst, ones[0:1, :], brow[0:1, a, :], start=False, stop=True)
            for d in range(CQ):
                dst = bank[2][:, 256 * d:256 * d + 256]
                pe.matmul(dst, ident[:], Fg[:, d, :], start=True, stop=False)
                for k in range(CQ):
                    pe.matmul(dst, neg[:], Fg[:, k, :], start=False, stop=False)
                pe.matmul(dst, ones[0:1, :], frow[0:1, 1, :], start=False, stop=True)
            for d in range(CQ):
                for e in range(CE):
                    pe.matmul(bank[3][:, 128 * d:128 * d + 128], WqT[2][:, e, 128 * d:128 * d + 128], WkT[2][:, e, :],
                              start=(e == 0), stop=(e == CE - 1))
            for e in range(CE):
                pe.matmul(bank[4][:, 0:256], bkrep[:, e, :], WqT[2][:, e, :], start=(e == 0), stop=(e == CE - 1))
            for e in range(CE):
                last = pe.matmul(bank[5][:, 0:256], WvT[2][:, e, :], Wo[2][:, e, :], start=(e == 0), stop=(e == CE - 1))
            last.then_inc(weights_centred, 1)
            pe.wait_ge(weights_ready, 1)

            def iteration(it, c):
                if live(it, c):
                    pe.wait_ge(in_normed, upto(it, c))
                    for d in range(CQ):
                        for b in range(PER):
                            at = 256 * d + 128 * b
                            last = pe.transpose(bank[0][:, at:at + 128], xn[c % 2][:, b, 128 * d:128 * d + 128], ident[:])
                    last.then_inc(xT_ready, 1)
                    for a in range(2):
                        for b in range(PER):
                            at = 256 * a + 128 * b
                            last = pe.transpose(bank[1][:, at:at + 128], yvn[c % 4][:, a, b, :], ident[:])
                    last.then_inc(yvT_ready, 1)
                if live(it, c - 3):
                    n = c - 3
                    pe.wait_ge(y1T_copied, upto(it, n))
                    pe.wait_ge(t1T_copied, upto(it, n))
                    if live(it, c - 2):
                        pe.wait_ge(o_added, upto(it, c - 2))
                    for b in range(PER):
                        at = slice(128 * b, 128 * b + 128)
                        last = pe.matmul(bank[2][:, at], t1T[:, at], y1T[n % 2][:, at], start=True, stop=True)
                    last.then_inc(s1_ready, 1)
                if live(it, c - 1):
                    pe.wait_ge(prob_normed, upto(it, c - 1))
                    for j in range(4):
                        last = pe.transpose(bank[3][:, 128 * j:128 * j + 128], prob[:, j, :], ident[:])
                    last.then_inc(probT_ready, 1)
                if live(it, c - 2):
                    pe.wait_ge(o_normed, upto(it, c - 2))
                    for d in range(CQ):
                        for b in range(PER):
                            at = 256 * d + 128 * b
                            last = pe.transpose(bank[4][:, at:at + 128], on[c % 2][:, b, 128 * d:128 * d + 128], ident[:])
                    last.then_inc(oT_ready, 1)
                if live(it, c):
                    pe.wait_ge(x_split, upto(it, c))
                    for a in range(2):
                        for d in range(CQ):
                            at = slice(256 * d, 256 * d + 256)
                            last = split(bank[5][:, 256 * a:256 * a + 256], Ahi[:, d, a, :], Alo[:, d, a, :],
                                         xhi[:, at], xlo[:, at], d == 0, d == CQ - 1)
                    last.then_inc(t_ready, 1)
                if live(it, c - 1):
                    pe.wait_ge(probT_copied, upto(it, c - 1))
                    for a in range(2):
                        for b in range(PER):
                            at = slice(256 * a + 128 * b, 256 * a + 128 * b + 128)
                            last = pe.matmul(bank[6][:, at], yvn[(c - 1) % 4][:, a, b, :], probT[:, at], start=True, stop=True)
                    last.then_inc(ctxT_ready, 1)
                if live(it, c - 3):
                    pe.wait_ge(prob1_normed, upto(it, c - 3))
                    if live(it, c - 4):
                        wait(pe, final_added, upto(it, c - 4))
                    for b in range(PER):
                        last = pe.transpose(bank[7][:, 128 * b:128 * b + 128], prob1[:, b, :], ident[:])
                    last.then_inc(prob1T_ready, 1)
                if live(it, c - 2):
                    pe.wait_ge(o_split, upto(it, c - 2))
                    for b in range(PER):
                        for d in range(CQ):
                            at = slice(256 * d + 128 * b, 256 * d + 128 * b + 128)
                            last = split(bank[0][:, 256 * b:256 * b + 256], ohi[:, at], olo[:, at],
                                         Fhi[:, d, :], Flo[:, d, :], d == 0, d == CQ - 1)
                    last.then_inc(fc_ready, 1)
                if live(it, c - 3):
                    n = c - 3
                    pe.wait_ge(prob1T_copied, upto(it, n))
                    if live(it, c):
                        pe.wait_ge(yvT_copied, upto(it, c))
                    for b in range(PER):
                        at = slice(128 * b, 128 * b + 128)
                        last = pe.matmul(bank[1][:, at], Y1[n % 4][:, b, :], prob1T[:, at], start=True, stop=True)
                    last.then_inc(ctx1T_ready, 1)
                if live(it, c - 1):
                    pe.wait_ge(c_split, upto(it, c - 1))
                    for b in range(PER):
                        for a in range(2):
                            at = slice(256 * a + 128 * b, 256 * a + 128 * b + 128)
                            last = split(bank[2][:, 256 * b:256 * b + 256], chi[:, at], clo[:, at],
                                         Whi[:, a, :], Wlo[:, a, :], a == 0, a == 1)
                    last.then_inc(proj_ready, 1)
                if live(it, c - 2):
                    n = c - 2
                    pe.wait_ge(y1_loaded[n % 4], nth(it, n, 4))
                    for b in range(PER):
                        pe.transpose(bank[4][:, 128 * b:128 * b + 128], Y1[n % 4][:, b, :], ident[:])
                    pe.wait_ge(x1_added, upto(it, n))
                    for d in range(CQ):
                        for b in range(PER):
                            at = 256 * d + 128 * b
                            last = pe.transpose(bank[3][:, at:at + 128], X1[n % 2][:, b, 128 * d:128 * d + 128], ident[:])
                    last.then_inc(x1T_ready, 1)
                if live(it, c):
                    pe.wait_ge(tT_copied, upto(it, c))
                    pe.wait_ge(yvT_copied, upto(it, c))
                    for j in range(4):
                        at = slice(128 * j, 128 * j + 128)
                        last = pe.matmul(bank[5][:, at], tT[:, at], yvT[:, at], start=True, stop=True)
                    last.then_inc(s_ready, 1)
                if live(it, c - 2):
                    pe.wait_ge(x1T_copied, upto(it, c - 2))
                    for d in range(CQ):
                        last = pe.matmul(bank[6][:, 0:256], M1[:, d, :], x1T[:, 256 * d:256 * d + 256],
                                         start=(d == 0), stop=(d == CQ - 1))
                    last.then_inc(t1_ready, 1)
                if live(it, c - 3):
                    pe.wait_ge(c1_split, upto(it, c - 3))
                    for b in range(PER):
                        at = slice(128 * b, 128 * b + 128)
                        last = split(bank[7][:, 256 * b:256 * b + 256], c1hi[:, at], c1lo[:, at],
                                     Whi[:, 2, :], Wlo[:, 2, :], True, True)
                    last.then_inc(proj1_ready, 1)

            run(pe, iteration, start=0)

        @block.vector
        def _(dve):
            def on_rows(t, n, length):
                return t[:, 0:n].unsqueeze(2).broadcast_to([128, n, length])

            def lo_part(dst, src, hi, s):
                dve.tensor_tensor(dst[:], src, hi[:].bitcast(F32), ALU.subtract).then_inc(s, 1)

            def read_stats(it, n):
                wait(dve, in_normed, upto(it, n - 2))
                dve.wait_ge(x_loaded[n % 4], nth(it, n, 4))
                for b in range(PER):
                    dve.bn_stats(inst[n % 2][:, b, :], X[n % 4][:, b, :])
                dve.wait_ge(yv_loaded[n % 2], nth(it, n, 2, 32))
                for a in range(2):
                    for b in range(PER):
                        last = dve.bn_stats(inst[n % 2][:, PER + PER * a + b, :], YV[n % 2][:, a, b, :])
                last.then_inc(in_stats, 1)

            read_stats(0, 0)

            dve.wait_ge(w_loaded, 16 * NLOADS)
            dve.tensor_scalar(g1s[:], col[:, G1:G1 + 4], SCALE, None, ALU.mult).then_inc(weights_step, 1)
            dve.tensor_copy(bkrep[:], on_rows(col[:, BK1:BK1 + 2], 2, 128)).then_inc(weights_step, 1)
            for d in range(CQ):
                dve.tensor_scalar(Fg[:, d, :], fcW[:, d, :], col[:, LNG + d:LNG + d + 1], None, ALU.mult).then_inc(weights_step, 1)
            dve.wait_ge(vecs_multiplied, 1)
            dve.tensor_tensor(vec[:], bank[0][:, 0:14], col[:, ADD:ADD + 14], ALU.add).then_inc(vecs_added, 1)
            dve.wait_ge(weights_multiplied, 1)
            for a in range(2):
                for d in range(CQ):
                    k = 2 * a + d
                    dve.tensor_tensor_reduce(U[:, k, :], bank[1 + a][:, 192 * d:192 * d + 128], g2b[:, a, :], 1.0, 0.0,
                                             ALU.mult, ALU.add, usum[:, k:k + 1]).then_inc(weights_step, 1)
                dve.tensor_tensor_reduce(Urow[0:1, a, :], bank[3][0:1, 192 * a:192 * a + 128], g2b[0:1, a, :], 1.0, 0.0,
                                         ALU.mult, ALU.add, usum[0:1, 4 + a:5 + a]).then_inc(weights_step, 1)
                dve.tensor_scalar(Wg[:, a, :], bank[4][:, 256 * a:256 * a + 256], col[:, G2 + a:G2 + a + 1], None,
                                  ALU.mult).then_inc(weights_step, 1)
                dve.tensor_tensor(brow[0:1, a, :], bank[6][0:1, 256 * a:256 * a + 256], row[0:1, a, :],
                                  ALU.add).then_inc(weights_step, 1)
            dve.tensor_tensor(qb1[:], col[:, BQ1:BQ1 + 2], bank[7][:, 0:2], ALU.subtract).then_inc(weights_step, 1)
            dve.tensor_tensor(frow[0:1, 0, :], bank[7][0:1, 256:512], row[0:1, 2, :], ALU.add).then_inc(weights_step, 1)
            dve.wait_ge(weights_step, 16)
            dve.tensor_tensor(frow[0:1, 1, :], frow[0:1, 0, :], row[0:1, 3, :], ALU.add).then_inc(weights_step, 1)
            for a in range(2):
                for d in range(CQ):
                    k = 2 * a + d
                    dve.scalar_tensor_tensor(out=usc[:, k:k + 1], in0=usum[:, k:k + 1], scalar=-1.0 / DK,
                                             in1=bank[1 + a][:, 192 * d + 128:192 * d + 129],
                                             op0=ALU.mult, op1=ALU.add).then_inc(weights_step, 1)
                dve.scalar_tensor_tensor(out=usc[0:1, 4 + a:5 + a], in0=usum[0:1, 4 + a:5 + a], scalar=-1.0 / DK,
                                         in1=bank[3][0:1, 192 * a + 128:192 * a + 129],
                                         op0=ALU.mult, op1=ALU.add).then_inc(weights_step, 1)
            dve.wait_ge(weights_step, 23)
            for a in range(2):
                for d in range(CQ):
                    k = 2 * a + d
                    dve.tensor_scalar(Af[:, d, a, :], U[:, k, :], usc[:, k:k + 1], g1s[:, k:k + 1],
                                      ALU.add, ALU.mult).then_inc(weights_step, 1)
                dve.tensor_scalar(crow[0:1, a, :], Urow[0:1, a, :], usc[0:1, 4 + a:5 + a], SCALE,
                                  ALU.add, ALU.mult).then_inc(weights_step, 1)
            dve.wait_ge(weights_step, 29)
            dve.tensor_copy(Ahi[:], Af[:]).then_inc(weights_scaled, 1)
            dve.wait_ge(weights_scaled, 1)
            dve.tensor_tensor(Alo[:], Af[:], Ahi[:].bitcast(F32), ALU.subtract)
            dve.wait_ge(weights_centred, 1)
            dve.tensor_copy(Whi[:, 0:2, :], bank[1][:].rearrange("p (a n) -> p a n", a=2)).then_inc(weights_step, 1)
            dve.tensor_copy(Whi[:, 2, :], bank[5][:, 0:256]).then_inc(weights_step, 1)
            dve.tensor_copy(Fhi[:], bank[2][:].rearrange("p (a n) -> p a n", a=2)).then_inc(weights_step, 1)
            dve.tensor_scalar(M1[:], bank[3][:, 0:256].rearrange("p (a n) -> p a n", a=2), SCALE, None, ALU.mult)
            dve.tensor_scalar(wr1[:], bank[4][:, 0:256], SCALE, None, ALU.mult)
            dve.tensor_copy(cc[:, 0:2], bank[0][:, 0:2])
            dve.tensor_scalar(cc[:, 2:4], bank[0][:, 2:4], SCALE, None, ALU.mult)
            dve.wait_ge(weights_step, 32)
            dve.tensor_tensor(Wlo[:, 0:2, :], bank[1][:].rearrange("p (a n) -> p a n", a=2),
                              Whi[:, 0:2, :].bitcast(F32), ALU.subtract)
            dve.tensor_tensor(Wlo[:, 2, :], bank[5][:, 0:256], Whi[:, 2, :].bitcast(F32), ALU.subtract)
            dve.tensor_tensor(Flo[:], bank[2][:].rearrange("p (a n) -> p a n", a=2),
                              Fhi[:].bitcast(F32), ALU.subtract).then_inc(weights_ready, 1)
            read_stats(0, 1)

            def iteration(it, c):
                if live(it, c - 3):
                    n = c - 3
                    dve.wait_ge(s1_ready, upto(it, n))
                    dve.tensor_reduce(max1[:], bank[2][:, 0:256].rearrange("p (b k) -> p b k", b=PER), AX.X,
                                      ALU.max).then_inc(max1_found, 1)
                    dve.wait_ge(max1_found, upto(it, n))
                    dve.wait_ge(r1_found, upto(it, n))
                    dve.tensor_tensor(top1[:], max1[:], r1[n % 2][:], ALU.add).then_inc(top1_found, 1)
                    dve.wait_ge(top1_found, upto(it, n))
                    dve.tensor_tensor(nmax1[:], r1[n % 2][:], top1[:], ALU.subtract).then_inc(nmax1_found, 1)
                if live(it, c):
                    dve.wait_ge(xhi_made, upto(it, c))
                    lo_part(xlo, bank[0][:], xhi, x_split)
                if live(it, c - 3):
                    dve.wait_ge(exp1_done, upto(it, c - 3))
                    dve.reciprocal(ri1[:], rs1[:]).then_inc(sum1_inverted, 1)
                    dve.wait_ge(sum1_inverted, upto(it, c - 3))
                    dve.tensor_tensor(prob1[:], prob1[:], on_rows(ri1, PER, 128), ALU.mult).then_inc(prob1_normed, 1)
                if live(it, c - 2):
                    dve.wait_ge(ohi_made, upto(it, c - 2))
                    lo_part(olo, bank[4][:], ohi, o_split)
                if live(it, c - 1):
                    dve.wait_ge(chi_made, upto(it, c - 1))
                    lo_part(clo, bank[6][:], chi, c_split)
                if live(it, c - 2):
                    n = c - 2
                    dve.wait_ge(fc_ready, upto(it, n))
                    dve.tensor_tensor(X1[n % 2][:], bank[0][:].rearrange("p (b n) -> p b n", b=PER), O[n % 2][:],
                                      ALU.add).then_inc(x1_added, 1)
                    dve.wait_ge(x1_added, upto(it, n))
                    for b in range(PER):
                        last = dve.tensor_tensor_reduce(junk[:, b, :], X1[n % 2][:, b, :], wr1[:], 1.0, cc[:, 3:4],
                                                        ALU.mult, ALU.add, r1[n % 2][:, b:b + 1])
                    last.then_inc(r1_found, 1)
                if live(it, c - 3):
                    dve.wait_ge(c1hi_made, upto(it, c - 3))
                    lo_part(c1lo, bank[1][:, 0:256], c1hi, c1_split)
                if live(it, c - 1):
                    n = c - 1
                    dve.wait_ge(proj_ready, upto(it, n))
                    dve.tensor_tensor(O[n % 2][:], bank[2][:].rearrange("p (b n) -> p b n", b=PER), X[n % 4][:],
                                      ALU.add).then_inc(o_added, 1)
                    dve.wait_ge(o_added, upto(it, n))
                    for b in range(PER):
                        last = dve.bn_stats(outst[n % 2][:, b, :], O[n % 2][:, b, :])
                    last.then_inc(out_stats, 1)
                if live(it, c):
                    dve.wait_ge(s_ready, upto(it, c))
                    dve.tensor_reduce(nmax[:], bank[5][:].rearrange("p (j k) -> p j k", j=4), AX.X, ALU.max,
                                      negate=True).then_inc(max_found, 1)
                if live(it, c + 2):
                    read_stats(it, c + 2)
                if live(it, c - 3):
                    n = c - 3
                    dve.wait_ge(proj1_ready, upto(it, n))
                    wait(dve, stored[n % 2], nth(it, n - 2, 2))
                    dve.tensor_tensor(fin[n % 2][:], bank[7][:].rearrange("p (b n) -> p b n", b=PER), X1[n % 2][:],
                                      ALU.add).then_inc(final_added, 1)
                if live(it, c):
                    dve.wait_ge(exp_done, upto(it, c))
                    dve.reciprocal(ri[:], rs[:]).then_inc(sum_inverted, 1)
                    dve.wait_ge(sum_inverted, upto(it, c))
                    dve.tensor_tensor(prob[:], prob[:], on_rows(ri, 4, 128), ALU.mult).then_inc(prob_normed, 1)

            run(dve, iteration, start=0)


NLOADS = 3 + 7 + 7 + 5 + 1


def kernel(**inputs):
    import numpy as _np
    import concourse.bacc as _bacc
    from concourse import mybir as _mybir
    from concourse.bass_utils import run_bass_kernel_spmd as _run

    def get(name):
        return _np.ascontiguousarray(inputs[name])

    def columns(name):
        return get(name).reshape(-1, 128).T

    def layout(a):
        return _np.ascontiguousarray(a)

    la, lv, l1 = "L0_xattn_a_", "L0_xattn_v_", "L1_xattn_"
    arrays = {"x": get("x"), "ctx": get("ctx_512"), "fside": get("fside_BxSxS_0")}
    for a, p in enumerate((la, lv, l1)):
        arrays[f"Wq{a}"] = get(p + "Wq")
        arrays[f"WqT{a}"] = layout(get(p + "Wq").T)
        if a < 2:
            arrays[f"Wk{a}"] = get(p + "Wk")
            arrays[f"Wv{a}"] = get(p + "Wv")
        arrays[f"WkT{a}"] = layout(get(p + "Wk").T)
        arrays[f"WvT{a}"] = layout(get(p + "Wv").T)
        arrays[f"Wo{a}"] = get(p + "Wo")
    arrays["fcW"] = get("L0_xattn_fc_W")
    arrays["cols"] = layout(_np.concatenate([columns(n) for n in (
        la + "bk", la + "bq", la + "bv", lv + "bk", lv + "bq", lv + "bv", l1 + "bo",
        la + "ln1_g", lv + "ln1_g", la + "ln1_b", lv + "ln1_b", la + "ln2_g", lv + "ln2_g", la + "ln2_b", lv + "ln2_b",
        "L0_xattn_ln_g", "L0_xattn_ln_b", l1 + "bq", l1 + "bk", l1 + "bv")], axis=1))
    arrays["rows"] = layout(_np.stack([get(la + "bo"), get(lv + "bo"), get("L0_xattn_fc_b"), get(l1 + "bo")])[None])
    arrays["g2rows"] = layout(_np.stack([get(la + "ln2_g"), get(lv + "ln2_g")]))

    nc = _bacc.Bacc("TRN2", target_bir_lowering=False, num_devices=1)
    aps = {name: nc.dram_tensor(f"in_{name}", a.shape, _mybir.dt.from_np(a.dtype), kind="ExternalInput").ap()
           for name, a in arrays.items()}
    out = nc.dram_tensor("out_0", (BATCH, SEQ, DQ), F32, kind="ExternalOutput").ap()
    build(nc, aps["x"], aps["ctx"], aps["fside"], aps, aps["cols"], aps["rows"], aps["g2rows"], out)
    r = _run(nc, [{f"in_{name}": a for name, a in arrays.items()}], core_ids=[0])
    return r.results[0]["out_0"]
```

```python
import concourse.bass as bass
from concourse import mybir
from contextlib import ExitStack

F32 = mybir.dt.float32
F32R = mybir.dt.float32r
ALU = mybir.AluOpType
ACT = mybir.ActivationFunctionType
AX = mybir.AxisListType

BATCH, SEQ, DQ, DK, E = 64, 128, 256, 128, 256
EPS = 1e-5
SCALE = float(E) ** -0.5
PER = 2
NG = BATCH // PER
CQ, CE = DQ // 128, E // 128
UNROLL = 4
FIRST = 6
LOOPS = (NG - 2 - FIRST) // UNROLL
LAST = NG + 2

BK, BQ, BV = 0, 6, 12
G1, G2 = 18, 22
LNG, LNB = 24, 26
NCOL = 28

B2_AT, G2_AT, B1_AT, BO1_AT, NROW = 0, 256, 512, 1024, 1280


def build(nc, x, ctx, ctxT, fside, w, cols, rows, wide_rows, out):
    with ExitStack() as stack:
        def sb(name, shape, dt=F32):
            return stack.enter_context(nc.sbuf_tensor(name, shape, dt))

        def sem(name):
            return stack.enter_context(nc.semaphore(name))

        WqT = [sb(f"WqT{a}", [128, CE, DQ]) for a in range(3)]
        WkT = [sb(f"WkT{a}", [128, CE, DK + 1]) for a in range(3)]
        WvT = [sb(f"WvT{a}", [128, CE, DK]) for a in range(3)]
        Wo = [sb(f"Wo{a}", [128, CE, DQ]) for a in range(3)]
        fcW = sb("fcW", [128, CQ, DQ])
        col = sb("col", [128, NCOL])
        row = sb("row", [1, 3, DQ])
        wide = sb("wide", [128, NROW])

        def b1(a):
            return wide[:, B1_AT + DQ * a:B1_AT + DQ * a + DQ]

        def b2(a):
            return wide[:, B2_AT + DK * a:B2_AT + DK * a + DK]

        def g2(a, parts=128):
            return wide[0:parts, G2_AT + DK * a:G2_AT + DK * a + DK]

        zeros = sb("zeros", [128, 128])
        ident = sb("ident", [128, 128])
        center = sb("center", [128, 128])
        neg = sb("neg", [128, 128])
        ones = sb("ones", [1, 128])
        nhalf = sb("nhalf", [128, 6])
        invn = sb("invn", [128, 6])
        shift = sb("shift", [128, 6])
        oshift = sb("oshift", [128, PER])
        half = sb("half", [128, 6])
        epsilon = sb("epsilon", [128, PER])

        scratch = sb("scratch", [128, 14, DQ])
        qb = sb("qb", [128, 2, CE])
        vb = sb("vb", [128, 2, CE])
        bias1 = sb("bias1", [128, DQ])
        g1s = sb("g1s", [128, 4])
        U = sb("U", [128, 4, DK])
        Urow = sb("Urow", [1, 2, DK])
        usum = sb("usum", [128, 6])
        usc = sb("usc", [128, 6])
        crow = sb("crow", [1, 2, DK])
        Wg = sb("Wg", [128, 2, DQ])
        brow = sb("brow", [1, 2, DQ])
        Fg = sb("Fg", [128, CQ, DQ])
        frow = sb("frow", [1, 2, DQ])
        qb1 = sb("qb1", [128, 2])
        bkrep = sb("bkrep", [128, CE, 128])
        bvrep = sb("bvrep", [128, CE, 128])
        Af = sb("Af", [128, CQ, 2, DK])
        Ahi, Alo = sb("Ahi", [128, CQ, 2, DK], F32R), sb("Alo", [128, CQ, 2, DK], F32R)
        Whi, Wlo = sb("Whi", [128, 3, DQ], F32R), sb("Wlo", [128, 3, DQ], F32R)
        Fhi, Flo = sb("Fhi", [128, CQ, DQ], F32R), sb("Flo", [128, CQ, DQ], F32R)
        M1 = sb("M1", [128, CQ, DK])
        wr1 = sb("wr1", [128, DQ])
        cc = sb("cc", [128, 4])

        X = [sb(f"X{k}", [128, PER, DQ]) for k in range(4)]
        YV = [sb(f"YV{k}", [128, 2, PER, DK]) for k in range(4)]
        Y1 = [sb(f"Y1{k}", [128, PER, DK]) for k in range(4)]
        inst = [sb(f"inst{k}", [128, 6, 6]) for k in range(2)]
        outst = [sb(f"outst{k}", [128, PER, 6]) for k in range(2)]
        inw = sb("inw", [128, 11, 6])
        outmv = [sb(f"outmv{k}", [128, PER, 2]) for k in range(2)]
        outw = sb("outw", [128, 4, PER])
        xn = [sb(f"xn{k}", [128, PER, DQ]) for k in range(2)]
        yvn = [sb(f"yvn{k}", [128, 2, PER, DK]) for k in range(4)]
        xhi, xlo = sb("xhi", [128, 512], F32R), sb("xlo", [128, 512], F32R)
        yvT = sb("yvT", [128, 512])
        tT = sb("tT", [128, 512])
        nmax = sb("nmax", [128, 4])
        rs = sb("rs", [128, 4])
        ri = sb("ri", [128, 4])
        prob = sb("prob", [128, 4, 128])
        probT = sb("probT", [128, 512])
        chi, clo = sb("chi", [128, 512], F32R), sb("clo", [128, 512], F32R)
        O = [sb(f"O{k}", [128, PER, DQ]) for k in range(2)]
        on = [sb(f"on{k}", [128, PER, DQ]) for k in range(2)]
        ohi, olo = sb("ohi", [128, 512], F32R), sb("olo", [128, 512], F32R)
        X1 = [sb(f"X1{k}", [128, PER, DQ]) for k in range(2)]
        junk = sb("junk", [128, PER, DQ])
        r1 = [sb(f"r1{k}", [128, PER]) for k in range(2)]
        x1T = sb("x1T", [128, 512])
        Y1T = [sb(f"Y1T{k}", [128, PER, SEQ]) for k in range(4)]
        t1T = sb("t1T", [128, 256])
        max1, top1, nmax1 = sb("max1", [128, PER]), sb("top1", [128, PER]), sb("nmax1", [128, PER])
        rs1, ri1 = sb("rs1", [128, PER]), sb("ri1", [128, PER])
        prob1 = sb("prob1", [128, PER, 128])
        prob1T = sb("prob1T", [128, 256])
        c1hi, c1lo = sb("c1hi", [128, 256], F32R), sb("c1lo", [128, 256], F32R)
        fin = [sb(f"fin{k}", [128, PER, DQ]) for k in range(2)]

        bank = [stack.enter_context(nc.psum_tensor(f"bank{k}", [128, 512], F32)) for k in range(8)]

        scores_w_loaded = sem("scores_w_loaded")
        k_vectors_loaded = sem("k_vectors_loaded")
        q_vectors_loaded = sem("q_vectors_loaded")
        values_w_loaded = sem("values_w_loaded")
        layer1_w_loaded = sem("layer1_w_loaded")
        consts_made = sem("consts_made")
        idents_made = sem("idents_made")
        weights_step = sem("weights_step")
        qk_multiplied = sem("qk_multiplied")
        kb_folded, kb_multiplied = sem("kb_folded"), sem("kb_multiplied")
        qb_folded, qb_multiplied = sem("qb_folded"), sem("qb_multiplied")
        A_ready = sem("A_ready")
        crow_made, c_turned, c_ready = sem("crow_made"), sem("c_turned"), sem("c_ready")
        vb_folded, vb_multiplied = sem("vb_folded"), sem("vb_multiplied")
        layer1_folded, layer1_multiplied = sem("layer1_folded"), sem("layer1_multiplied")
        W_scaled, W_centred = sem("W_scaled"), sem("W_centred")
        F_scaled, F_centred, F_ready = sem("F_scaled"), sem("F_centred"), sem("F_ready")
        x_loaded = [sem(f"x_loaded{k}") for k in range(4)]
        yv_loaded = [sem(f"yv_loaded{k}") for k in range(4)]
        y1_loaded = [sem(f"y1_loaded{k}") for k in range(4)]
        stored = [sem(f"stored{k}") for k in range(2)]
        in_stats = sem("in_stats")
        in_step = sem("in_step")
        x_normed, yv_normed = sem("x_normed"), sem("yv_normed")
        scalars_awaited = sem("scalars_awaited")
        xT_ready, yvT_ready = sem("xT_ready"), sem("yvT_ready")
        xhi_made, x_split, yvT_copied = sem("xhi_made"), sem("x_split"), sem("yvT_copied")
        t_ready, tT_copied = sem("t_ready"), sem("tT_copied")
        s_ready, max_found, exp_done = sem("s_ready"), sem("max_found"), sem("exp_done")
        sum_inverted, prob_normed = sem("sum_inverted"), sem("prob_normed")
        probT_ready, probT_copied = sem("probT_ready"), sem("probT_copied")
        ctxT_ready, chi_made, c_split = sem("ctxT_ready"), sem("chi_made"), sem("c_split")
        proj_ready, o_added = sem("proj_ready"), sem("o_added")
        out_stats, out_aggregated = sem("out_stats"), sem("out_aggregated")
        out_step, o_normed = sem("out_step"), sem("o_normed")
        oT_ready, ohi_made, o_split = sem("oT_ready"), sem("ohi_made"), sem("o_split")
        fc_ready, x1_added, r1_found = sem("fc_ready"), sem("x1_added"), sem("r1_found")
        x1T_ready, x1T_copied = sem("x1T_ready"), sem("x1T_copied")
        t1_ready, t1T_copied = sem("t1_ready"), sem("t1T_copied")
        s1_ready, max1_found, top1_found, nmax1_found = sem("s1_ready"), sem("max1_found"), sem("top1_found"), sem("nmax1_found")
        exp1_done, sum1_inverted = sem("exp1_done"), sem("sum1_inverted")
        prob1T_ready, prob1T_copied = sem("prob1T_ready"), sem("prob1T_copied")
        ctx1T_ready, c1hi_made, c1_split = sem("ctx1T_ready"), sem("c1hi_made"), sem("c1_split")
        proj1_ready, final_added = sem("proj1_ready"), sem("final_added")

        block = stack.enter_context(nc.Block())

        x_g = x.rearrange("(g b) q d -> g q b d", b=PER)
        ctx_g = ctx.rearrange("(g b) q d -> g q b d", b=PER)
        ctxT_g = ctxT.rearrange("(g b) d q -> g d b q", b=PER)
        fside_g = fside.rearrange("(g b) q d -> g q b d", b=PER)
        out_g = out.rearrange("(g b) q d -> g q b d", b=PER)

        def live(it, c):
            return not isinstance(it, int) or 0 <= UNROLL * it + c < NG

        def upto(it, c, k=1):
            return it * (UNROLL * k) + k * (c + 1)

        def nth(it, c, slots, k=16):
            return it * (k * UNROLL // slots) + k * (c // slots + 1)

        def wait(eng, s, value):
            if not isinstance(value, int) or value > 0:
                eng.wait_ge(s, value)

        def run(eng, iteration, start=-2, last=LAST):
            for c in range(start, FIRST):
                iteration(0, c)
            with eng.Fori(0, LOOPS) as it:
                for c in range(FIRST, FIRST + UNROLL):
                    iteration(it, c)
            for c in range(FIRST, last + 1 - UNROLL * LOOPS):
                iteration(LOOPS, c)

        @block.sync
        def _(sp):
            def iteration(it, c):
                g = it * UNROLL + c
                if live(it, c - 1):
                    n = c - 1
                    wait(sp, ctx1T_ready, upto(it, n - 4))
                    sp.dma_start(Y1[n % 4][:], ctx_g[g - 1]).then_inc(y1_loaded[n % 4], 16)
                    sp.dma_start(Y1T[n % 4][:], ctxT_g[g - 1]).then_inc(y1_loaded[n % 4], 16)
                if live(it, c - 5):
                    n = c - 5
                    sp.wait_ge(final_added, upto(it, n))
                    sp.dma_start(out_g[g - 5], fin[n % 2][:]).then_inc(stored[n % 2], 16)
                if isinstance(it, int) and it == 0 and c == 0:
                    sp.wait_ge(kb_folded, 1)
                if live(it, c + 2):
                    n = c + 2
                    wait(sp, yv_normed, upto(it, n - 4))
                    sp.dma_start(YV[n % 4][:, 0], ctx_g[g + 2]).then_inc(yv_loaded[n % 4], 16)
                    sp.dma_start(YV[n % 4][:, 1], fside_g[g + 2]).then_inc(yv_loaded[n % 4], 16)
                    wait(sp, o_added, upto(it, n - 4))
                    sp.dma_start(X[n % 4][:], x_g[g + 2]).then_inc(x_loaded[n % 4], 16)

            run(sp, iteration, last=LAST + 2)
            for k in range(2):
                sp.wait_ge(stored[k], 16 * NG // 2)

        @block.gpsimd
        def _(pool):
            pool.memset(zeros[:], 0.0).then_inc(consts_made, 1)
            pool.memset(neg[:], -1.0 / DQ).then_inc(consts_made, 1)
            pool.memset(center[:], -1.0 / DK).then_inc(consts_made, 1)
            pool.memset(ones[:], 1.0).then_inc(consts_made, 1)
            pool.memset(nhalf[:], -0.5).then_inc(consts_made, 1)
            pool.memset(invn[:, 0:PER], 1.0 / DQ).then_inc(consts_made, 1)
            pool.memset(invn[:, PER:6], 1.0 / DK).then_inc(consts_made, 1)
            pool.memset(shift[:, 0:PER], 0.0).then_inc(consts_made, 1)
            pool.memset(shift[:, PER:6], 1.0 / DK).then_inc(consts_made, 1)
            pool.memset(oshift[:], 1.0 / DQ).then_inc(consts_made, 1)
            pool.memset(half[:], 0.5).then_inc(consts_made, 1)
            pool.memset(epsilon[:], EPS).then_inc(consts_made, 1)
            pool.wait_ge(consts_made, 12)
            pool.affine_select(out=ident[:], in_=zeros[:], compare_op=ALU.not_equal, fill=1.0, base=0,
                               pattern=[[-1, 128]], channel_multiplier=1).then_inc(idents_made, 1)
            pool.affine_select(out=center[:], in_=center[:], compare_op=ALU.not_equal, fill=1.0 - 1.0 / DK, base=0,
                               pattern=[[-1, 128]], channel_multiplier=1).then_inc(idents_made, 1)

            def before_scalars(value_ready, value):
                pool.wait_ge(value_ready, value)
                pool.sem_inc(scalars_awaited, 1)

            STEPS, OSTEPS = 11, 4

            def input_scales(it, n):
                def made(k):
                    pool.wait_ge(in_step, upto(it, n - 1, STEPS) + k)

                st, wk = inst[n % 2], inw
                me, mo, se, so = st[:, :, 1], st[:, :, 4], st[:, :, 2], st[:, :, 5]
                pool.tensor_tensor(wk[:, 0, :], me, mo, ALU.add).then_inc(in_step, 1)
                pool.tensor_tensor(wk[:, 1, :], me, mo, ALU.subtract).then_inc(in_step, 1)
                pool.tensor_tensor(wk[:, 2, :], se, so, ALU.add).then_inc(in_step, 1)
                made(2)
                pool.tensor_tensor(wk[:, 3, :], wk[:, 1, :], wk[:, 1, :], ALU.mult).then_inc(in_step, 1)
                made(3)
                pool.tensor_tensor(wk[:, 4, :], wk[:, 2, :], invn[:], ALU.mult).then_inc(in_step, 1)
                pool.tensor_tensor(wk[:, 8, :], wk[:, 0, :], half[:], ALU.mult).then_inc(in_step, 1)
                before_scalars(in_step, upto(it, n - 1, STEPS) + 4)
                pool.tensor_scalar(wk[:, 5, :], wk[:, 3, :], 0.25, EPS, ALU.mult, ALU.add).then_inc(in_step, 1)
                made(7)
                pool.tensor_tensor(wk[:, 6, :], wk[:, 4, :], wk[:, 5, :], ALU.add).then_inc(in_step, 1)
                made(8)
                pool.tensor_tensor(wk[:, 7, :], wk[:, 6, :], nhalf[:], ALU.pow).then_inc(in_step, 1)
                made(9)
                pool.tensor_tensor(wk[:, 10, :], wk[:, 8, :], wk[:, 7, :], ALU.mult).then_inc(in_step, 1)
                made(10)
                pool.tensor_tensor(wk[:, 9, :], shift[:], wk[:, 10, :], ALU.subtract).then_inc(in_step, 1)

            def output_scales(it, n):
                def made(k):
                    pool.wait_ge(out_step, upto(it, n - 1, OSTEPS) + k)

                mv, wk = outmv[n % 2], outw
                pool.tensor_tensor(wk[:, 0, :], mv[:, :, 1], epsilon[:], ALU.add).then_inc(out_step, 1)
                made(1)
                pool.tensor_tensor(wk[:, 1, :], wk[:, 0, :], nhalf[:, 0:PER], ALU.pow).then_inc(out_step, 1)
                made(2)
                pool.tensor_tensor(wk[:, 2, :], mv[:, :, 0], wk[:, 1, :], ALU.mult).then_inc(out_step, 1)
                made(3)
                pool.tensor_tensor(wk[:, 3, :], oshift[:], wk[:, 2, :], ALU.subtract).then_inc(out_step, 1)

            def iteration(it, c):
                if live(it, c - 2):
                    n = c - 2
                    pool.wait_ge(out_aggregated, upto(it, n))
                    output_scales(it, n)
                    wait(pool, oT_ready, upto(it, n - 2))
                    before_scalars(out_step, upto(it, n, OSTEPS))
                    for b in range(PER):
                        last = pool.tensor_scalar(on[n % 2][:, b, :], O[n % 2][:, b, :], outw[:, 1, b:b + 1],
                                                  outw[:, 3, b:b + 1], ALU.mult, ALU.add)
                    last.then_inc(o_normed, 1)
                if live(it, c + 1):
                    n = c + 1
                    pool.wait_ge(in_stats, upto(it, n))
                    input_scales(it, n)
                    wait(pool, xT_ready, upto(it, n - 2))
                    wait(pool, ctxT_ready, upto(it, n - 4))
                    before_scalars(in_step, upto(it, n, STEPS))
                    for b in range(PER):
                        last = pool.tensor_scalar(xn[n % 2][:, b, :], X[n % 4][:, b, :], inw[:, 7, b:b + 1], inw[:, 9, b:b + 1],
                                                  ALU.mult, ALU.add)
                    last.then_inc(x_normed, 1)
                    for a in range(2):
                        for b in range(PER):
                            j = PER + PER * a + b
                            last = pool.tensor_scalar(yvn[n % 4][:, a, b, :], YV[n % 4][:, a, b, :], inw[:, 7, j:j + 1],
                                                      inw[:, 9, j:j + 1], ALU.mult, ALU.add)
                    last.then_inc(yv_normed, 1)

            run(pool, iteration, last=LAST)

        @block.scalar
        def _(act):
            def load(dst, src, s):
                act.dma_start(dst, src).then_inc(s, 16)

            def chunks(name):
                return w[name].rearrange("(c p) n -> p c n", p=128)

            for a in range(2):
                load(WkT[a][:, :, 0:DK], chunks(f"WkT{a}"), scores_w_loaded)
                load(WqT[a][:], chunks(f"WqT{a}"), scores_w_loaded)
            load(wide[:, 0:B1_AT], wide_rows[0:B1_AT].partition_broadcast(128), k_vectors_loaded)
            load(col[:], cols, k_vectors_loaded)
            load(wide[:, B1_AT:NROW], wide_rows[B1_AT:NROW].partition_broadcast(128), q_vectors_loaded)
            for a in range(2):
                load(WvT[a][:], chunks(f"WvT{a}"), values_w_loaded)
                load(Wo[a][:], chunks(f"Wo{a}"), values_w_loaded)
            load(row[:], rows, layer1_w_loaded)
            load(WvT[2][:], chunks("WvT2"), layer1_w_loaded)
            load(Wo[2][:], chunks("Wo2"), layer1_w_loaded)
            load(WkT[2][:, :, 0:DK], chunks("WkT2"), layer1_w_loaded)
            load(WqT[2][:], chunks("WqT2"), layer1_w_loaded)
            load(fcW[:], chunks("fcW"), layer1_w_loaded)

            def copy(dst, src, s):
                act.activation(dst, src, ACT.Copy).then_inc(s, 1)

            def iteration(it, c):
                if live(it, c - 3):
                    act.wait_ge(x1T_ready, upto(it, c - 3))
                    copy(x1T[:], bank[3][:], x1T_copied)
                if live(it, c):
                    act.wait_ge(xT_ready, upto(it, c))
                    copy(xhi[:], bank[0][:], xhi_made)
                if live(it, c):
                    act.wait_ge(yvT_ready, upto(it, c))
                    copy(yvT[:], bank[1][:], yvT_copied)
                if live(it, c - 1):
                    act.wait_ge(probT_ready, upto(it, c - 1))
                    copy(probT[:], bank[3][:], probT_copied)
                if live(it, c):
                    act.wait_ge(t_ready, upto(it, c))
                    if isinstance(it, int) and it == 0 and c == 0:
                        act.wait_ge(c_ready, 1)
                    for a in range(2):
                        last = act.activation(tT[:, 256 * a:256 * a + 256], bank[5][:, 256 * a:256 * a + 256],
                                              ACT.Identity, bias=cc[:, a:a + 1], scale=1.0)
                    last.then_inc(tT_copied, 1)
                if live(it, c - 2):
                    act.wait_ge(oT_ready, upto(it, c - 2))
                    copy(ohi[:], bank[4][:], ohi_made)
                if live(it, c - 3):
                    act.wait_ge(nmax1_found, upto(it, c - 3))
                    for b in range(PER):
                        last = act.activation(prob1[:, b, :], bank[2][:, 128 * b:128 * b + 128], ACT.Exp,
                                              bias=nmax1[:, b:b + 1], scale=1.0, accum_out=rs1[:, b:b + 1])
                    last.then_inc(exp1_done, 1)
                if live(it, c - 1):
                    act.wait_ge(ctxT_ready, upto(it, c - 1))
                    copy(chi[:], bank[6][:], chi_made)
                if live(it, c - 3):
                    act.wait_ge(prob1T_ready, upto(it, c - 3))
                    copy(prob1T[:], bank[7][:, 0:256], prob1T_copied)
                if live(it, c):
                    act.wait_ge(max_found, upto(it, c))
                    for j in range(4):
                        last = act.activation(prob[:, j, :], bank[5][:, 128 * j:128 * j + 128], ACT.Exp,
                                              bias=nmax[:, j:j + 1], scale=1.0, accum_out=rs[:, j:j + 1])
                    last.then_inc(exp_done, 1)
                if live(it, c - 3):
                    act.wait_ge(ctx1T_ready, upto(it, c - 3))
                    copy(c1hi[:], bank[1][:, 0:256], c1hi_made)

            run(act, iteration, start=0)

        @block.tensor
        def _(pe):
            def split(dst, hi, lo, rhi, rlo, first, last):
                pe.matmul(dst, hi, rhi, start=first, stop=False)
                pe.matmul(dst, hi, rlo, start=False, stop=False)
                return pe.matmul(dst, lo, rhi, start=False, stop=last)

            def product(dst, lhsT, rhs):
                for e in range(CE):
                    last = pe.matmul(dst, lhsT(e), rhs(e), start=(e == 0), stop=(e == CE - 1))
                return last

            def x_turned(it, c):
                pe.wait_ge(x_normed, upto(it, c))
                for d in range(CQ):
                    for b in range(PER):
                        at = 256 * d + 128 * b
                        last = pe.transpose(bank[0][:, at:at + 128], xn[c % 2][:, b, 128 * d:128 * d + 128], ident[:])
                last.then_inc(xT_ready, 1)

            def yv_turned(it, c):
                pe.wait_ge(yv_normed, upto(it, c))
                for a in range(2):
                    for b in range(PER):
                        at = 256 * a + 128 * b
                        last = pe.transpose(bank[1][:, at:at + 128], yvn[c % 4][:, a, b, :], ident[:])
                last.then_inc(yvT_ready, 1)

            def queries(it, c):
                pe.wait_ge(x_split, upto(it, c))
                for a in range(2):
                    for d in range(CQ):
                        at = slice(256 * d, 256 * d + 256)
                        last = split(bank[5][:, 256 * a:256 * a + 256], Ahi[:, d, a, :], Alo[:, d, a, :],
                                     xhi[:, at], xlo[:, at], d == 0, d == CQ - 1)
                last.then_inc(t_ready, 1)

            def scores(it, c):
                pe.wait_ge(tT_copied, upto(it, c))
                pe.wait_ge(yvT_copied, upto(it, c))
                for j in range(4):
                    at = slice(128 * j, 128 * j + 128)
                    last = pe.matmul(bank[5][:, at], tT[:, at], yvT[:, at], start=True, stop=True)
                last.then_inc(s_ready, 1)

            def iteration(it, c):
                if live(it, c):
                    x_turned(it, c)
                if live(it, c - 4):
                    pe.wait_ge(c1_split, upto(it, c - 4))
                    for b in range(PER):
                        at = slice(128 * b, 128 * b + 128)
                        last = split(bank[7][:, 256 * b:256 * b + 256], c1hi[:, at], c1lo[:, at],
                                     Whi[:, 2, :], Wlo[:, 2, :], True, True)
                    last.then_inc(proj1_ready, 1)
                if live(it, c - 3):
                    pe.wait_ge(x1T_copied, upto(it, c - 3))
                    for d in range(CQ):
                        last = pe.matmul(bank[6][:, 0:256], M1[:, d, :], x1T[:, 256 * d:256 * d + 256],
                                         start=(d == 0), stop=(d == CQ - 1))
                    last.then_inc(t1_ready, 1)
                if live(it, c):
                    yv_turned(it, c)
                if live(it, c - 1):
                    pe.wait_ge(prob_normed, upto(it, c - 1))
                    for j in range(4):
                        last = pe.transpose(bank[3][:, 128 * j:128 * j + 128], prob[:, j, :], ident[:])
                    last.then_inc(probT_ready, 1)
                if live(it, c):
                    queries(it, c)
                if live(it, c - 3):
                    n = c - 3
                    pe.wait_ge(y1_loaded[n % 4], nth(it, n, 4, 32))
                    pe.wait_ge(t1T_copied, upto(it, n))
                    if live(it, c - 2):
                        pe.wait_ge(o_added, upto(it, c - 2))
                    for b in range(PER):
                        at = slice(128 * b, 128 * b + 128)
                        last = pe.matmul(bank[2][:, at], t1T[:, at], Y1T[n % 4][:, b, :], start=True, stop=True)
                    last.then_inc(s1_ready, 1)
                if live(it, c - 2):
                    pe.wait_ge(o_normed, upto(it, c - 2))
                    for d in range(CQ):
                        for b in range(PER):
                            at = 256 * d + 128 * b
                            last = pe.transpose(bank[4][:, at:at + 128], on[c % 2][:, b, 128 * d:128 * d + 128], ident[:])
                    last.then_inc(oT_ready, 1)
                if live(it, c - 1):
                    pe.wait_ge(probT_copied, upto(it, c - 1))
                    if isinstance(it, int) and it == 0 and c == 1:
                        pe.wait_ge(F_ready, 1)
                    for a in range(2):
                        for b in range(PER):
                            at = slice(256 * a + 128 * b, 256 * a + 128 * b + 128)
                            last = pe.matmul(bank[6][:, at], yvn[(c - 1) % 4][:, a, b, :], probT[:, at], start=True, stop=True)
                    last.then_inc(ctxT_ready, 1)
                if live(it, c):
                    scores(it, c)
                if live(it, c - 3):
                    pe.wait_ge(exp1_done, upto(it, c - 3))
                    if live(it, c - 4):
                        wait(pe, final_added, upto(it, c - 4))
                    for b in range(PER):
                        last = pe.transpose(bank[7][:, 128 * b:128 * b + 128], prob1[:, b, :], ident[:])
                    last.then_inc(prob1T_ready, 1)
                if live(it, c - 2):
                    pe.wait_ge(o_split, upto(it, c - 2))
                    for b in range(PER):
                        for d in range(CQ):
                            at = slice(256 * d + 128 * b, 256 * d + 128 * b + 128)
                            last = split(bank[0][:, 256 * b:256 * b + 256], ohi[:, at], olo[:, at],
                                         Fhi[:, d, :], Flo[:, d, :], d == 0, d == CQ - 1)
                    last.then_inc(fc_ready, 1)
                if live(it, c - 3):
                    n = c - 3
                    pe.wait_ge(prob1T_copied, upto(it, n))
                    if live(it, c):
                        pe.wait_ge(yvT_copied, upto(it, c))
                    for b in range(PER):
                        at = slice(128 * b, 128 * b + 128)
                        last = pe.matmul(bank[1][:, at], Y1[n % 4][:, b, :], prob1T[:, at], start=True, stop=True)
                    last.then_inc(ctx1T_ready, 1)
                if live(it, c - 1):
                    pe.wait_ge(c_split, upto(it, c - 1))
                    for b in range(PER):
                        for a in range(2):
                            at = slice(256 * a + 128 * b, 256 * a + 128 * b + 128)
                            last = split(bank[2][:, 256 * b:256 * b + 256], chi[:, at], clo[:, at],
                                         Whi[:, a, :], Wlo[:, a, :], a == 0, a == 1)
                    last.then_inc(proj_ready, 1)
                if live(it, c - 2):
                    n = c - 2
                    pe.wait_ge(x1_added, upto(it, n))
                    for d in range(CQ):
                        for b in range(PER):
                            at = 256 * d + 128 * b
                            last = pe.transpose(bank[3][:, at:at + 128], X1[n % 2][:, b, 128 * d:128 * d + 128], ident[:])
                    last.then_inc(x1T_ready, 1)

            pe.wait_ge(scores_w_loaded, 16 * 4)
            for a in range(2):
                for d in range(CQ):
                    last = product(bank[1 + a][:, 128 * d:128 * d + 128], lambda e: WqT[a][:, e, 128 * d:128 * d + 128],
                                   lambda e: WkT[a][:, e, 0:DK])
            last.then_inc(qk_multiplied, 1)
            pe.wait_ge(kb_folded, 1)
            for a in range(2):
                for d in range(CQ):
                    k = 2 * a + d
                    last = product(bank[3][:, k:k + 1], lambda e: WqT[a][:, e, 128 * d:128 * d + 128],
                                   lambda e: WkT[a][:, e, DK:DK + 1])
            last.then_inc(kb_multiplied, 1)
            pe.wait_ge(values_w_loaded, 16 * 4)
            for a in range(2):
                product(bank[4][:, 256 * a:256 * a + 256], lambda e: WvT[a][:, e, :], lambda e: Wo[a][:, e, :])
            pe.wait_ge(qb_folded, 1)
            for a in range(2):
                last = product(bank[6][0:1, 192 * a:192 * a + 129], lambda e: qb[:, a, e:e + 1], lambda e: WkT[a][:, e, :])
            last.then_inc(qb_multiplied, 1)
            pe.wait_ge(idents_made, 2)
            pe.wait_ge(A_ready, 1)
            x_turned(0, 0)
            yv_turned(0, 0)
            pe.wait_ge(layer1_w_loaded, 16 * 6)
            product(bank[3][:, 256:512], lambda e: WvT[2][:, e, :], lambda e: Wo[2][:, e, :])
            for d in range(CQ):
                product(bank[2][:, 256 + 128 * d:384 + 128 * d], lambda e: WqT[2][:, e, 128 * d:128 * d + 128],
                        lambda e: WkT[2][:, e, 0:DK])
            queries(0, 0)
            pe.wait_ge(crow_made, 1)
            for a in range(2):
                last = pe.matmul(bank[7][:, a:a + 1], crow[0:1, a, :], ones[0:1, 0:1], start=True, stop=True)
            last.then_inc(c_turned, 1)
            pe.wait_ge(vb_folded, 1)
            for a in range(2):
                last = product(bank[6][0:1, 256 * a:256 * a + 256], lambda e: vb[:, a, e:e + 1], lambda e: Wo[a][:, e, :])
            last.then_inc(vb_multiplied, 1)
            pe.wait_ge(layer1_folded, 1)
            pe.wait_ge(c_ready, 1)
            product(bank[7][:, 256:512], lambda e: bvrep[:, e, :], lambda e: Wo[2][:, e, :])
            product(bank[2][:, 0:256], lambda e: bkrep[:, e, :], lambda e: WqT[2][:, e, :])
            product(bank[3][0:1, 0:256], lambda e: col[:, LNB + e:LNB + e + 1],
                    lambda e: fcW[:, e, :]).then_inc(layer1_multiplied, 1)
            scores(0, 0)
            pe.wait_ge(W_scaled, 1)
            for a in range(2):
                dst = bank[4][:, 256 * a:256 * a + 256]
                pe.matmul(dst, center[:], Wg[:, a, :], start=True, stop=False)
                last = pe.matmul(dst, ones[0:1, :], brow[0:1, a, :], start=False, stop=True)
            last.then_inc(W_centred, 1)
            pe.wait_ge(F_scaled, 1)
            for d in range(CQ):
                dst = bank[6][:, 256 * d:256 * d + 256]
                pe.matmul(dst, ident[:], Fg[:, d, :], start=True, stop=False)
                for k in range(CQ):
                    pe.matmul(dst, neg[:], Fg[:, k, :], start=False, stop=False)
                pe.matmul(dst, ones[0:1, :], frow[0:1, 1, :], start=False, stop=True)
            product(bank[7][:, 0:1], lambda e: WkT[2][:, e, 0:DK], lambda e: qb1[:, e:e + 1])
            product(bank[7][:, 1:2], lambda e: bkrep[:, e, :], lambda e: qb1[:, e:e + 1]).then_inc(F_centred, 1)

            run(pe, iteration, start=1, last=LAST + 1)

        @block.vector
        def _(dve):
            def on_rows(t, n, length):
                return t[:, 0:n].unsqueeze(2).broadcast_to([128, n, length])

            def lo_part(dst, src, hi, s):
                dve.tensor_tensor(dst[:], src, hi[:].bitcast(F32), ALU.subtract).then_inc(s, 1)

            def x_stats(it, n):
                dve.wait_ge(x_loaded[n % 4], nth(it, n, 4))
                for b in range(PER):
                    last = dve.bn_stats(inst[n % 2][:, b, :], X[n % 4][:, b, :])
                last.then_inc(in_stats, 1)

            def yv_stats(it, n):
                wait(dve, yv_normed, upto(it, n - 2))
                dve.wait_ge(yv_loaded[n % 4], nth(it, n, 4, 32))
                for a in range(2):
                    for b in range(PER):
                        dve.bn_stats(inst[n % 2][:, PER + PER * a + b, :], YV[n % 4][:, a, b, :])

            def x_rest(it, c):
                dve.wait_ge(xhi_made, upto(it, c))
                lo_part(xlo, bank[0][:], xhi, x_split)

            def largest(it, c):
                dve.wait_ge(s_ready, upto(it, c))
                dve.tensor_reduce(nmax[:], bank[5][:].rearrange("p (j k) -> p j k", j=4), AX.X, ALU.max,
                                  negate=True).then_inc(max_found, 1)

            def row_sums(k, mat, vector, begin, dst, scale=1.0):
                return dve.tensor_tensor_reduce(scratch[:, k, 0:vector.shape[-1]], mat, vector, scale, begin,
                                                ALU.mult, ALU.add, dst)

            def halves(t):
                return t.rearrange("p (a n) -> p a n", a=2)

            def iteration(it, c):
                if live(it, c - 2):
                    n = c - 2
                    dve.wait_ge(proj_ready, upto(it, n))
                    dve.tensor_tensor(O[n % 2][:], halves(bank[2][:]), X[n % 4][:], ALU.add).then_inc(o_added, 1)
                    dve.wait_ge(o_added, upto(it, n))
                    for b in range(PER):
                        last = dve.bn_stats(outst[n % 2][:, b, :], O[n % 2][:, b, :])
                    last.then_inc(out_stats, 1)
                if live(it, c - 2):
                    dve.wait_ge(out_stats, upto(it, c - 2))
                if live(it, c - 1):
                    n = c - 1
                    dve.wait_ge(exp_done, upto(it, n))
                    dve.reciprocal(ri[:], rs[:]).then_inc(sum_inverted, 1)
                if live(it, c - 2):
                    n = c - 2
                    for b in range(PER):
                        last = dve.bn_aggr(outmv[n % 2][:, b, :], outst[n % 2][:, b, :])
                    last.then_inc(out_aggregated, 1)
                if live(it, c - 1):
                    n = c - 1
                    dve.wait_ge(sum_inverted, upto(it, n))
                    dve.tensor_tensor(prob[:], prob[:], on_rows(ri, 4, 128), ALU.mult).then_inc(prob_normed, 1)
                if live(it, c):
                    x_rest(it, c)
                if live(it, c - 3):
                    dve.wait_ge(t1_ready, upto(it, c - 3))
                    dve.tensor_scalar(t1T[:], bank[6][:, 0:256], cc[:, 2:3], None, ALU.add).then_inc(t1T_copied, 1)
                if live(it, c - 3):
                    n = c - 3
                    dve.wait_ge(x1_added, upto(it, n))
                    for b in range(PER):
                        last = dve.tensor_tensor_reduce(junk[:, b, :], X1[n % 2][:, b, :], wr1[:], 1.0, cc[:, 3:4],
                                                        ALU.mult, ALU.add, r1[n % 2][:, b:b + 1])
                    last.then_inc(r1_found, 1)
                if live(it, c - 4):
                    n = c - 4
                    dve.wait_ge(proj1_ready, upto(it, n))
                    dve.wait_ge(sum1_inverted, upto(it, n))
                    wait(dve, stored[n % 2], nth(it, n - 2, 2))
                    for b in range(PER):
                        last = dve.scalar_tensor_tensor(out=fin[n % 2][:, b, :], in0=bank[7][:, 256 * b:256 * b + 256],
                                                        scalar=ri1[:, b:b + 1], in1=X1[n % 2][:, b, :],
                                                        op0=ALU.mult, op1=ALU.add)
                    last.then_inc(final_added, 1)
                if live(it, c - 3):
                    dve.wait_ge(s1_ready, upto(it, c - 3))
                    dve.tensor_reduce(max1[:], bank[2][:, 0:256].rearrange("p (b k) -> p b k", b=PER), AX.X,
                                      ALU.max).then_inc(max1_found, 1)
                if live(it, c - 3):
                    n = c - 3
                    dve.wait_ge(max1_found, upto(it, n))
                    dve.wait_ge(r1_found, upto(it, n))
                    dve.tensor_tensor(top1[:], max1[:], r1[n % 2][:], ALU.add).then_inc(top1_found, 1)
                    dve.wait_ge(top1_found, upto(it, n))
                    dve.tensor_tensor(nmax1[:], r1[n % 2][:], top1[:], ALU.subtract).then_inc(nmax1_found, 1)
                if live(it, c + 2):
                    yv_stats(it, c + 2)
                if live(it, c - 2):
                    dve.wait_ge(ohi_made, upto(it, c - 2))
                    lo_part(olo, bank[4][:], ohi, o_split)
                if live(it, c):
                    largest(it, c)
                if live(it, c - 3):
                    dve.wait_ge(exp1_done, upto(it, c - 3))
                    if live(it, c - 4):
                        dve.wait_ge(final_added, upto(it, c - 4))
                    dve.reciprocal(ri1[:], rs1[:]).then_inc(sum1_inverted, 1)
                if live(it, c - 1):
                    dve.wait_ge(chi_made, upto(it, c - 1))
                    lo_part(clo, bank[6][:], chi, c_split)
                if live(it, c - 2):
                    n = c - 2
                    dve.wait_ge(fc_ready, upto(it, n))
                    dve.tensor_tensor(X1[n % 2][:], halves(bank[0][:]), O[n % 2][:], ALU.add).then_inc(x1_added, 1)
                if live(it, c + 2):
                    x_stats(it, c + 2)
                if live(it, c - 3):
                    dve.wait_ge(c1hi_made, upto(it, c - 3))
                    lo_part(c1lo, bank[1][:, 0:256], c1hi, c1_split)

            yv_stats(0, 0)
            x_stats(0, 0)
            dve.wait_ge(scores_w_loaded, 16 * 4)
            dve.wait_ge(k_vectors_loaded, 16 * 2)
            for k in range(4):
                a, e = k // 2, k % 2
                last = row_sums(k, WkT[a][:, e, 0:DK], b2(a), col[:, BK + k:BK + k + 1], WkT[a][:, e, DK:DK + 1])
            last.then_inc(kb_folded, 1)
            dve.tensor_scalar(g1s[:], col[:, G1:G1 + 4], SCALE, None, ALU.mult).then_inc(weights_step, 1)
            dve.wait_ge(qk_multiplied, 1)
            for k in range(4):
                a, d = k // 2, k % 2
                dve.tensor_tensor_reduce(U[:, k, :], bank[1 + a][:, 128 * d:128 * d + 128], g2(a), 1.0, 0.0,
                                         ALU.mult, ALU.add, usum[:, k:k + 1]).then_inc(weights_step, 1)
            dve.wait_ge(kb_multiplied, 1)
            dve.wait_ge(weights_step, 5)
            dve.scalar_tensor_tensor(out=usc[:, 0:4], in0=usum[:, 0:4], scalar=-1.0 / DK, in1=bank[3][:, 0:4],
                                     op0=ALU.mult, op1=ALU.add).then_inc(weights_step, 1)
            dve.wait_ge(weights_step, 6)
            for k in range(4):
                a, d = k // 2, k % 2
                dve.tensor_scalar(Af[:, d, a, :], U[:, k, :], usc[:, k:k + 1], g1s[:, k:k + 1],
                                  ALU.add, ALU.mult).then_inc(weights_step, 1)
            dve.wait_ge(weights_step, 10)
            dve.tensor_copy(Ahi[:], Af[:]).then_inc(weights_step, 1)
            dve.wait_ge(weights_step, 11)
            dve.tensor_tensor(Alo[:], Af[:], Ahi[:].bitcast(F32), ALU.subtract).then_inc(A_ready, 1)
            dve.wait_ge(q_vectors_loaded, 16)
            for k in range(4):
                a, e = k // 2, k % 2
                last = row_sums(4 + k, WqT[a][:, e, :], b1(a), col[:, BQ + k:BQ + k + 1], qb[:, a, e:e + 1])
            last.then_inc(qb_folded, 1)
            yv_stats(0, 1)
            x_stats(0, 1)
            x_rest(0, 0)
            dve.wait_ge(qb_multiplied, 1)
            for a in range(2):
                dve.tensor_tensor_reduce(Urow[0:1, a, :], bank[6][0:1, 192 * a:192 * a + 128], g2(a, 1), 1.0, 0.0,
                                         ALU.mult, ALU.add, usum[0:1, 4 + a:5 + a]).then_inc(weights_step, 1)
            dve.wait_ge(weights_step, 13)
            for a in range(2):
                dve.scalar_tensor_tensor(out=usc[0:1, 4 + a:5 + a], in0=usum[0:1, 4 + a:5 + a], scalar=-1.0 / DK,
                                         in1=bank[6][0:1, 192 * a + 128:192 * a + 129],
                                         op0=ALU.mult, op1=ALU.add).then_inc(weights_step, 1)
            dve.wait_ge(weights_step, 15)
            for a in range(2):
                last = dve.tensor_scalar(crow[0:1, a, :], Urow[0:1, a, :], usc[0:1, 4 + a:5 + a], SCALE,
                                         ALU.add, ALU.mult)
            last.then_inc(crow_made, 1)
            dve.wait_ge(values_w_loaded, 16 * 4)
            for k in range(4):
                a, e = k // 2, k % 2
                last = row_sums(8 + k, WvT[a][:, e, :], b2(a), col[:, BV + k:BV + k + 1], vb[:, a, e:e + 1])
            last.then_inc(vb_folded, 1)
            dve.wait_ge(c_turned, 1)
            dve.tensor_copy(cc[:, 0:2], bank[7][:, 0:2]).then_inc(c_ready, 1)
            dve.tensor_copy(bkrep[:], on_rows(col[:, BK + 4:BK + 6], CE, 128))
            dve.tensor_copy(bvrep[:], on_rows(col[:, BV + 4:BV + 6], CE, 128)).then_inc(layer1_folded, 1)
            dve.wait_ge(vb_multiplied, 1)
            for a in range(2):
                dve.tensor_tensor(brow[0:1, a, :], bank[6][0:1, 256 * a:256 * a + 256], row[0:1, a, :], ALU.add)
                last = dve.tensor_scalar(Wg[:, a, :], bank[4][:, 256 * a:256 * a + 256], col[:, G2 + a:G2 + a + 1], None,
                                         ALU.mult)
            last.then_inc(W_scaled, 1)
            yv_stats(0, 2)
            dve.wait_ge(layer1_w_loaded, 16 * 6)
            for d in range(CQ):
                dve.tensor_scalar(Fg[:, d, :], fcW[:, d, :], col[:, LNG + d:LNG + d + 1], None, ALU.mult)
            dve.wait_ge(layer1_multiplied, 1)
            dve.tensor_tensor(bias1[:], bank[7][:, 256:512], wide[:, BO1_AT:BO1_AT + DQ], ALU.add).then_inc(weights_step, 1)
            dve.tensor_tensor(frow[0:1, 0, :], bank[3][0:1, 0:256], row[0:1, 2, :], ALU.add).then_inc(weights_step, 1)
            largest(0, 0)
            dve.wait_ge(weights_step, 17)
            dve.tensor_tensor(frow[0:1, 1, :], frow[0:1, 0, :], bias1[0:1, :], ALU.add)
            for e in range(CE):
                last = row_sums(12 + e, WqT[2][:, e, :], bias1[:], col[:, BQ + 4 + e:BQ + 5 + e], qb1[:, e:e + 1], -1.0)
            last.then_inc(F_scaled, 1)
            dve.wait_ge(W_centred, 1)
            dve.tensor_copy(Whi[:, 0:2, :], halves(bank[4][:])).then_inc(weights_step, 1)
            dve.tensor_copy(Whi[:, 2, :], bank[3][:, 256:512]).then_inc(weights_step, 1)
            dve.wait_ge(weights_step, 18)
            dve.tensor_tensor(Wlo[:, 0:2, :], halves(bank[4][:]), Whi[:, 0:2, :].bitcast(F32), ALU.subtract)
            dve.wait_ge(weights_step, 19)
            dve.tensor_tensor(Wlo[:, 2, :], bank[3][:, 256:512], Whi[:, 2, :].bitcast(F32), ALU.subtract)
            dve.tensor_scalar(wr1[:], bank[2][:, 0:256], SCALE, None, ALU.mult)
            dve.tensor_scalar(M1[:], halves(bank[2][:, 256:512]), SCALE, None, ALU.mult)
            dve.wait_ge(F_centred, 1)
            dve.tensor_copy(Fhi[:], halves(bank[6][:])).then_inc(weights_step, 1)
            dve.tensor_scalar(cc[:, 2:4], bank[7][:, 0:2], SCALE, None, ALU.mult)
            dve.wait_ge(weights_step, 20)
            dve.tensor_tensor(Flo[:], halves(bank[6][:]), Fhi[:].bitcast(F32), ALU.subtract).then_inc(F_ready, 1)
            x_stats(0, 2)
            run(dve, iteration, start=1, last=LAST + 1)


def kernel(**inputs):
    import numpy as _np
    import concourse.bacc as _bacc
    from concourse import mybir as _mybir
    from concourse.bass_utils import run_bass_kernel_spmd as _run

    def get(name):
        return _np.ascontiguousarray(inputs[name])

    def columns(name):
        return get(name).reshape(-1, 128).T

    def layout(a):
        return _np.ascontiguousarray(a)

    la, lv, l1 = "L0_xattn_a_", "L0_xattn_v_", "L1_xattn_"
    arrays = {"x": get("x"), "ctx": get("ctx_512"), "ctxT": layout(get("ctx_512").transpose(0, 2, 1)),
              "fside": get("fside_BxSxS_0")}
    for a, p in enumerate((la, lv, l1)):
        arrays[f"WqT{a}"] = layout(get(p + "Wq").T)
        arrays[f"WkT{a}"] = layout(get(p + "Wk").T)
        arrays[f"WvT{a}"] = layout(get(p + "Wv").T)
        arrays[f"Wo{a}"] = get(p + "Wo")
    arrays["fcW"] = get("L0_xattn_fc_W")
    arrays["cols"] = layout(_np.concatenate([columns(n) for n in (
        la + "bk", lv + "bk", l1 + "bk", la + "bq", lv + "bq", l1 + "bq", la + "bv", lv + "bv", l1 + "bv",
        la + "ln1_g", lv + "ln1_g", la + "ln2_g", lv + "ln2_g", "L0_xattn_ln_g", "L0_xattn_ln_b")], axis=1))
    arrays["rows"] = layout(_np.stack([get(la + "bo"), get(lv + "bo"), get("L0_xattn_fc_b")])[None])
    arrays["wide_rows"] = layout(_np.concatenate([get(n) for n in (
        la + "ln2_b", lv + "ln2_b", la + "ln2_g", lv + "ln2_g", la + "ln1_b", lv + "ln1_b", l1 + "bo")]))

    nc = _bacc.Bacc("TRN2", target_bir_lowering=False, num_devices=1)
    aps = {name: nc.dram_tensor(f"in_{name}", a.shape, _mybir.dt.from_np(a.dtype), kind="ExternalInput").ap()
           for name, a in arrays.items()}
    out = nc.dram_tensor("out_0", (BATCH, SEQ, DQ), F32, kind="ExternalOutput").ap()
    build(nc, aps["x"], aps["ctx"], aps["ctxT"], aps["fside"], aps, aps["cols"], aps["rows"], aps["wide_rows"], out)
    r = _run(nc, [{f"in_{name}": a for name, a in arrays.items()}], core_ids=[0])
    return r.results[0]["out_0"]
```

```python
import concourse.bass as bass
from concourse import mybir
from contextlib import ExitStack

F32 = mybir.dt.float32
F32R = mybir.dt.float32r
ALU = mybir.AluOpType
ACT = mybir.ActivationFunctionType
AX = mybir.AxisListType

BATCH, SEQ, DQ, DK, E = 64, 128, 256, 128, 256
EPS = 1e-5
SCALE = float(E) ** -0.5
PER = 2
NG = BATCH // PER
CQ, CE = DQ // 128, E // 128
UNROLL = 4
FIRST = 6
LOOPS = (NG - 2 - FIRST) // UNROLL
LAST = NG + 2

BK, BQ, BV = 0, 6, 12
G1, G2 = 18, 22
LNG, LNB = 24, 26
NCOL = 28

B2_AT, G2_AT, B1_AT, BO1_AT, NROW = 0, 256, 512, 1024, 1280


def build(nc, x, ctx, ctxT, fside, w, cols, rows, wide_rows, out):
    with ExitStack() as stack:
        def sb(name, shape, dt=F32):
            return stack.enter_context(nc.sbuf_tensor(name, shape, dt))

        def sem(name):
            return stack.enter_context(nc.semaphore(name))

        WqT = [sb(f"WqT{a}", [128, CE, DQ]) for a in range(3)]
        WkT = [sb(f"WkT{a}", [128, CE, DK + 1]) for a in range(3)]
        WvT = [sb(f"WvT{a}", [128, CE, DK]) for a in range(3)]
        Wo = [sb(f"Wo{a}", [128, CE, DQ]) for a in range(3)]
        fcW = sb("fcW", [128, CQ, DQ])
        col = sb("col", [128, NCOL])
        row = sb("row", [1, 3, DQ])
        wide = sb("wide", [128, NROW])

        def b1(a):
            return wide[:, B1_AT + DQ * a:B1_AT + DQ * a + DQ]

        def b2(a):
            return wide[:, B2_AT + DK * a:B2_AT + DK * a + DK]

        def g2(a, parts=128):
            return wide[0:parts, G2_AT + DK * a:G2_AT + DK * a + DK]

        zeros = sb("zeros", [128, 128])
        ident = sb("ident", [128, 128])
        center = sb("center", [128, 128])
        neg = sb("neg", [128, 128])
        ones = sb("ones", [1, 128])
        nhalf = sb("nhalf", [128, 6])
        invn = sb("invn", [128, 6])
        shift = sb("shift", [128, 6])
        oshift = sb("oshift", [128, PER])
        half = sb("half", [128, 6])
        epsilon = sb("epsilon", [128, PER])
        expo = sb("expo", [128, PER])

        scratch = sb("scratch", [128, 14, DQ])
        qb = sb("qb", [128, 2, CE])
        vb = sb("vb", [128, 2, CE])
        bias1 = sb("bias1", [128, DQ])
        g1s = sb("g1s", [128, 4])
        U = sb("U", [128, 4, DK])
        Urow = sb("Urow", [1, 2, DK])
        usum = sb("usum", [128, 6])
        usc = sb("usc", [128, 6])
        crow = sb("crow", [1, 2, DK])
        Wg = sb("Wg", [128, 2, DQ])
        brow = sb("brow", [1, 2, DQ])
        Fg = sb("Fg", [128, CQ, DQ])
        Ff = sb("Ff", [128, CQ, DQ])
        frow = sb("frow", [1, 2, DQ])
        qb1 = sb("qb1", [128, 2])
        bkrep = sb("bkrep", [128, CE, 128])
        bvrep = sb("bvrep", [128, CE, 128])
        Af = sb("Af", [128, CQ, 2, DK])
        Ahi, Alo = sb("Ahi", [128, CQ, 2, DK], F32R), sb("Alo", [128, CQ, 2, DK], F32R)
        Whi, Wlo = sb("Whi", [128, 3, DQ], F32R), sb("Wlo", [128, 3, DQ], F32R)
        Fhi, Flo = sb("Fhi", [128, CQ, DQ], F32R), sb("Flo", [128, CQ, DQ], F32R)
        M1 = sb("M1", [128, CQ, DK])
        M1hi, M1lo = sb("M1hi", [128, CQ, DK], F32R), sb("M1lo", [128, CQ, DK], F32R)
        wr1 = sb("wr1", [128, DQ])
        cc = sb("cc", [128, 4])

        X = [sb(f"X{k}", [128, PER, DQ]) for k in range(4)]
        YV = [sb(f"YV{k}", [128, 2, PER, DK]) for k in range(4)]
        Y1 = [sb(f"Y1{k}", [128, PER, DK]) for k in range(4)]
        inst = [sb(f"inst{k}", [128, 6, 6]) for k in range(2)]
        outst = [sb(f"outst{k}", [128, PER, 6]) for k in range(2)]
        inw = sb("inw", [128, 11, 6])
        outmv = [sb(f"outmv{k}", [128, PER, 2]) for k in range(2)]
        outw = sb("outw", [128, 4, PER])
        xn = [sb(f"xn{k}", [128, PER, DQ]) for k in range(2)]
        yvn = [sb(f"yvn{k}", [128, 2, PER, DK]) for k in range(4)]
        xhi, xlo = sb("xhi", [128, 512], F32R), sb("xlo", [128, 512], F32R)
        yvT = sb("yvT", [128, 512])
        tT = sb("tT", [128, 512])
        nmax = sb("nmax", [128, 4])
        rs = sb("rs", [128, 4])
        ri = sb("ri", [128, 4])
        prob = sb("prob", [128, 4, 128])
        probT = sb("probT", [128, 512])
        chi, clo = sb("chi", [128, 512], F32R), sb("clo", [128, 512], F32R)
        O = [sb(f"O{k}", [128, PER, DQ]) for k in range(2)]
        on = [sb(f"on{k}", [128, PER, DQ]) for k in range(2)]
        ohi, olo = sb("ohi", [128, 512], F32R), sb("olo", [128, 512], F32R)
        X1 = [sb(f"X1{k}", [128, PER, DQ]) for k in range(2)]
        junk = sb("junk", [128, PER, DQ])
        r1 = [sb(f"r1{k}", [128, PER]) for k in range(2)]
        x1hi, x1lo = sb("x1hi", [128, 512], F32R), sb("x1lo", [128, 512], F32R)
        Y1T = [sb(f"Y1T{k}", [128, PER, SEQ]) for k in range(4)]
        t1T = sb("t1T", [128, 256])
        max1, top1, nmax1 = sb("max1", [128, PER]), sb("top1", [128, PER]), sb("nmax1", [128, PER])
        rs1, ri1 = sb("rs1", [128, PER]), sb("ri1", [128, PER])
        prob1 = sb("prob1", [128, PER, 128])
        prob1T = sb("prob1T", [128, 256])
        c1hi, c1lo = sb("c1hi", [128, 256], F32R), sb("c1lo", [128, 256], F32R)
        fin = [sb(f"fin{k}", [128, PER, DQ]) for k in range(2)]

        bank = [stack.enter_context(nc.psum_tensor(f"bank{k}", [128, 512], F32)) for k in range(8)]

        scores_w_loaded = sem("scores_w_loaded")
        keys_w_loaded = sem("keys_w_loaded")
        q_vectors_loaded = sem("q_vectors_loaded")
        values_w_loaded = sem("values_w_loaded")
        layer1_w_loaded = sem("layer1_w_loaded")
        consts_made = sem("consts_made")
        idents_made = sem("idents_made")
        weights_step = sem("weights_step")
        qk_multiplied = sem("qk_multiplied")
        kb_folded = sem("kb_folded")
        qb_folded, qb_multiplied = sem("qb_folded"), sem("qb_multiplied")
        A_ready = sem("A_ready")
        crow_made, c_turned, c_ready = sem("crow_made"), sem("c_turned"), sem("c_ready")
        vb_folded, vb_multiplied = sem("vb_folded"), sem("vb_multiplied")
        layer1_paired = sem("layer1_paired")
        layer1_folded = sem("layer1_folded")
        offsets_multiplied = sem("offsets_multiplied")
        wr1_multiplied = sem("wr1_multiplied")
        weights_copied = sem("weights_copied")
        W1_ready = sem("W1_ready")
        W_scaled, W_centred, W_ready = sem("W_scaled"), sem("W_centred"), sem("W_ready")
        F_scaled, F_averaged, F_ready = sem("F_scaled"), sem("F_averaged"), sem("F_ready")
        x_loaded = [sem(f"x_loaded{k}") for k in range(4)]
        yv_loaded = [sem(f"yv_loaded{k}") for k in range(4)]
        y1_loaded = [sem(f"y1_loaded{k}") for k in range(4)]
        stored = [sem(f"stored{k}") for k in range(2)]
        in_stats = sem("in_stats")
        in_step = sem("in_step")
        x_normed, yv_normed = sem("x_normed"), sem("yv_normed")
        scalars_awaited = sem("scalars_awaited")
        xT_ready, yvT_ready = sem("xT_ready"), sem("yvT_ready")
        xhi_made, x_split, yvT_copied = sem("xhi_made"), sem("x_split"), sem("yvT_copied")
        t_ready, tT_copied = sem("t_ready"), sem("tT_copied")
        s_ready, max_found, exp_done = sem("s_ready"), sem("max_found"), sem("exp_done")
        sum_inverted, prob_normed = sem("sum_inverted"), sem("prob_normed")
        probT_ready, probT_copied = sem("probT_ready"), sem("probT_copied")
        ctxT_ready, chi_made, c_split = sem("ctxT_ready"), sem("chi_made"), sem("c_split")
        proj_ready, o_added = sem("proj_ready"), sem("o_added")
        out_stats, out_aggregated = sem("out_stats"), sem("out_aggregated")
        out_step, o_normed = sem("out_step"), sem("o_normed")
        oT_ready, ohi_made, o_split = sem("oT_ready"), sem("ohi_made"), sem("o_split")
        fc_ready, x1_added, r1_found = sem("fc_ready"), sem("x1_added"), sem("r1_found")
        x1T_ready, x1hi_made, x1_split = sem("x1T_ready"), sem("x1hi_made"), sem("x1_split")
        t1_ready, t1T_copied = sem("t1_ready"), sem("t1T_copied")
        s1_ready, max1_found, top1_found, nmax1_found = sem("s1_ready"), sem("max1_found"), sem("top1_found"), sem("nmax1_found")
        exp1_done, sum1_inverted = sem("exp1_done"), sem("sum1_inverted")
        prob1T_ready, prob1T_copied = sem("prob1T_ready"), sem("prob1T_copied")
        ctx1T_ready, c1hi_made, c1_split = sem("ctx1T_ready"), sem("c1hi_made"), sem("c1_split")
        proj1_ready, final_added = sem("proj1_ready"), sem("final_added")

        block = stack.enter_context(nc.Block())

        x_g = x.rearrange("(g b) q d -> g q b d", b=PER)
        ctx_g = ctx.rearrange("(g b) q d -> g q b d", b=PER)
        ctxT_g = ctxT.rearrange("(g b) d q -> g d b q", b=PER)
        fside_g = fside.rearrange("(g b) q d -> g q b d", b=PER)
        out_g = out.rearrange("(g b) q d -> g q b d", b=PER)

        def live(it, c):
            return not isinstance(it, int) or 0 <= UNROLL * it + c < NG

        def at_group(it, c, n):
            return isinstance(it, int) and UNROLL * it + c == n

        def upto(it, c, k=1):
            return it * (UNROLL * k) + k * (c + 1)

        def nth(it, c, slots, k=16):
            return it * (k * UNROLL // slots) + k * (c // slots + 1)

        def wait(eng, s, value):
            if not isinstance(value, int) or value > 0:
                eng.wait_ge(s, value)

        def run(eng, iteration, start=-2, last=LAST):
            for c in range(start, FIRST):
                iteration(0, c)
            with eng.Fori(0, LOOPS) as it:
                for c in range(FIRST, FIRST + UNROLL):
                    iteration(it, c)
            for c in range(FIRST, last + 1 - UNROLL * LOOPS):
                iteration(LOOPS, c)

        def chunks(name):
            return w[name].rearrange("(c p) n -> p c n", p=128)

        @block.sync
        def _(sp):
            def iteration(it, c):
                g = it * UNROLL + c
                if live(it, c - 1):
                    n = c - 1
                    wait(sp, ctx1T_ready, upto(it, n - 4))
                    sp.dma_start(Y1[n % 4][:], ctx_g[g - 1]).then_inc(y1_loaded[n % 4], 16)
                    sp.dma_start(Y1T[n % 4][:], ctxT_g[g - 1]).then_inc(y1_loaded[n % 4], 16)
                if live(it, c - 5):
                    n = c - 5
                    sp.wait_ge(final_added, upto(it, n))
                    sp.dma_start(out_g[g - 5], fin[n % 2][:]).then_inc(stored[n % 2], 16)
                if live(it, c + 2):
                    n = c + 2
                    wait(sp, yv_normed, upto(it, n - 4))
                    sp.dma_start(YV[n % 4][:, 0], ctx_g[g + 2]).then_inc(yv_loaded[n % 4], 16)
                    sp.dma_start(YV[n % 4][:, 1], fside_g[g + 2]).then_inc(yv_loaded[n % 4], 16)
                    wait(sp, o_added, upto(it, n - 4))
                    sp.dma_start(X[n % 4][:], x_g[g + 2]).then_inc(x_loaded[n % 4], 16)

            iteration(0, -2)
            for a in range(2):
                sp.dma_start(WqT[a][:], chunks(f"WqT{a}")).then_inc(scores_w_loaded, 16)
            iteration(0, -1)
            sp.dma_start(row[:], rows).then_inc(layer1_w_loaded, 16)
            sp.dma_start(WvT[2][:], chunks("WvT2")).then_inc(layer1_w_loaded, 16)
            sp.dma_start(Wo[2][:], chunks("Wo2")).then_inc(layer1_w_loaded, 16)
            sp.dma_start(WkT[2][:, :, 0:DK], chunks("WkT2")).then_inc(layer1_w_loaded, 16)
            sp.dma_start(WqT[2][:], chunks("WqT2")).then_inc(layer1_w_loaded, 16)
            sp.dma_start(fcW[:], chunks("fcW")).then_inc(layer1_w_loaded, 16)
            run(sp, iteration, start=0, last=LAST + 2)
            for k in range(2):
                sp.wait_ge(stored[k], 16 * NG // 2)

        @block.gpsimd
        def _(pool):
            pool.memset(zeros[:], 0.0).then_inc(consts_made, 1)
            pool.memset(neg[:], -1.0 / DQ).then_inc(consts_made, 1)
            pool.memset(center[:], -1.0 / DK).then_inc(consts_made, 1)
            pool.memset(ones[:], 1.0).then_inc(consts_made, 1)
            pool.memset(nhalf[:], -0.5).then_inc(consts_made, 1)
            pool.memset(invn[:, 0:PER], 1.0 / DQ).then_inc(consts_made, 1)
            pool.memset(invn[:, PER:6], 1.0 / DK).then_inc(consts_made, 1)
            pool.memset(shift[:, 0:PER], 0.0).then_inc(consts_made, 1)
            pool.memset(shift[:, PER:6], 1.0 / DK).then_inc(consts_made, 1)
            pool.memset(oshift[:], 1.0 / DQ).then_inc(consts_made, 1)
            pool.memset(half[:], 0.5).then_inc(consts_made, 1)
            pool.memset(epsilon[:], EPS).then_inc(consts_made, 1)
            pool.wait_ge(consts_made, 12)
            pool.affine_select(out=ident[:], in_=zeros[:], compare_op=ALU.not_equal, fill=1.0, base=0,
                               pattern=[[-1, 128]], channel_multiplier=1).then_inc(idents_made, 1)
            pool.affine_select(out=center[:], in_=center[:], compare_op=ALU.not_equal, fill=1.0 - 1.0 / DK, base=0,
                               pattern=[[-1, 128]], channel_multiplier=1).then_inc(idents_made, 1)

            def before_scalars(value_ready, value):
                pool.wait_ge(value_ready, value)
                pool.sem_inc(scalars_awaited, 1)

            STEPS, OSTEPS = 11, 4

            def input_scales(it, n):
                def made(k):
                    pool.wait_ge(in_step, upto(it, n - 1, STEPS) + k)

                st, wk = inst[n % 2], inw
                me, mo, se, so = st[:, :, 1], st[:, :, 4], st[:, :, 2], st[:, :, 5]
                pool.tensor_tensor(wk[:, 0, :], me, mo, ALU.add).then_inc(in_step, 1)
                pool.tensor_tensor(wk[:, 1, :], me, mo, ALU.subtract).then_inc(in_step, 1)
                pool.tensor_tensor(wk[:, 2, :], se, so, ALU.add).then_inc(in_step, 1)
                made(2)
                pool.tensor_tensor(wk[:, 3, :], wk[:, 1, :], wk[:, 1, :], ALU.mult).then_inc(in_step, 1)
                made(3)
                pool.tensor_tensor(wk[:, 4, :], wk[:, 2, :], invn[:], ALU.mult).then_inc(in_step, 1)
                pool.tensor_tensor(wk[:, 8, :], wk[:, 0, :], half[:], ALU.mult).then_inc(in_step, 1)
                before_scalars(in_step, upto(it, n - 1, STEPS) + 4)
                pool.tensor_scalar(wk[:, 5, :], wk[:, 3, :], 0.25, EPS, ALU.mult, ALU.add).then_inc(in_step, 1)
                made(7)
                pool.tensor_tensor(wk[:, 6, :], wk[:, 4, :], wk[:, 5, :], ALU.add).then_inc(in_step, 1)
                made(8)
                pool.tensor_tensor(wk[:, 7, :], wk[:, 6, :], nhalf[:], ALU.pow).then_inc(in_step, 1)
                made(9)
                pool.tensor_tensor(wk[:, 10, :], wk[:, 8, :], wk[:, 7, :], ALU.mult).then_inc(in_step, 1)
                made(10)
                pool.tensor_tensor(wk[:, 9, :], shift[:], wk[:, 10, :], ALU.subtract).then_inc(in_step, 1)

            def output_scales(it, n):
                def made(k):
                    pool.wait_ge(out_step, upto(it, n - 1, OSTEPS) + k)

                mv, wk = outmv[n % 2], outw
                pool.tensor_tensor(wk[:, 0, :], mv[:, :, 1], epsilon[:], ALU.add).then_inc(out_step, 1)
                made(1)
                pool.tensor_tensor(wk[:, 1, :], wk[:, 0, :], nhalf[:, 0:PER], ALU.pow).then_inc(out_step, 1)
                made(2)
                pool.tensor_tensor(wk[:, 2, :], mv[:, :, 0], wk[:, 1, :], ALU.mult).then_inc(out_step, 1)
                made(3)
                pool.tensor_tensor(wk[:, 3, :], oshift[:], wk[:, 2, :], ALU.subtract).then_inc(out_step, 1)

            def iteration(it, c):
                if live(it, c - 2):
                    n = c - 2
                    pool.wait_ge(out_aggregated, upto(it, n))
                    output_scales(it, n)
                    wait(pool, oT_ready, upto(it, n - 2))
                    before_scalars(out_step, upto(it, n, OSTEPS))
                    for b in range(PER):
                        last = pool.tensor_scalar(on[n % 2][:, b, :], O[n % 2][:, b, :], outw[:, 1, b:b + 1],
                                                  outw[:, 3, b:b + 1], ALU.mult, ALU.add)
                    last.then_inc(o_normed, 1)
                if live(it, c + 1):
                    n = c + 1
                    pool.wait_ge(in_stats, upto(it, n))
                    input_scales(it, n)
                    wait(pool, xT_ready, upto(it, n - 2))
                    wait(pool, ctxT_ready, upto(it, n - 4))
                    before_scalars(in_step, upto(it, n, STEPS))
                    for b in range(PER):
                        last = pool.tensor_scalar(xn[n % 2][:, b, :], X[n % 4][:, b, :], inw[:, 7, b:b + 1], inw[:, 9, b:b + 1],
                                                  ALU.mult, ALU.add)
                    last.then_inc(x_normed, 1)
                    for a in range(2):
                        for b in range(PER):
                            j = PER + PER * a + b
                            last = pool.tensor_scalar(yvn[n % 4][:, a, b, :], YV[n % 4][:, a, b, :], inw[:, 7, j:j + 1],
                                                      inw[:, 9, j:j + 1], ALU.mult, ALU.add)
                    last.then_inc(yv_normed, 1)

            run(pool, iteration, last=LAST)

        @block.scalar
        def _(act):
            def load(dst, src, s):
                act.dma_start(dst, src).then_inc(s, 16)

            load(wide[:, 0:B1_AT], wide_rows[0:B1_AT].partition_broadcast(128), keys_w_loaded)
            for a in range(2):
                load(WkT[a][:, :, 0:DK], chunks(f"WkT{a}"), keys_w_loaded)
            load(col[:], cols, keys_w_loaded)
            load(wide[:, B1_AT:NROW], wide_rows[B1_AT:NROW].partition_broadcast(128), q_vectors_loaded)
            for a in range(2):
                load(WvT[a][:], chunks(f"WvT{a}"), values_w_loaded)
                load(Wo[a][:], chunks(f"Wo{a}"), values_w_loaded)
            act.wait_ge(consts_made, 12)
            act.activation(expo[:], epsilon[:], ACT.Exp)

            def copy(dst, src, s):
                act.activation(dst, src, ACT.Copy).then_inc(s, 1)

            def iteration(it, c):
                if live(it, c - 4):
                    act.wait_ge(ctx1T_ready, upto(it, c - 4))
                    copy(c1hi[:], bank[1][:, 0:256], c1hi_made)
                if live(it, c):
                    act.wait_ge(xT_ready, upto(it, c))
                    copy(xhi[:], bank[2][:], xhi_made)
                if live(it, c - 3):
                    act.wait_ge(x1T_ready, upto(it, c - 3))
                    copy(x1hi[:], bank[3][:], x1hi_made)
                if live(it, c):
                    act.wait_ge(yvT_ready, upto(it, c))
                    copy(yvT[:], bank[4][:], yvT_copied)
                if live(it, c - 1):
                    act.wait_ge(probT_ready, upto(it, c - 1))
                    copy(probT[:], bank[7][:], probT_copied)
                if live(it, c - 3):
                    act.wait_ge(t1_ready, upto(it, c - 3))
                    act.activation(t1T[:], bank[7][:, 0:256], ACT.Identity, bias=cc[:, 2:3],
                                   scale=1.0).then_inc(t1T_copied, 1)
                if live(it, c):
                    act.wait_ge(t_ready, upto(it, c))
                    if at_group(it, c, 0):
                        act.wait_ge(c_ready, 1)
                    for a in range(2):
                        last = act.activation(tT[:, 256 * a:256 * a + 256], bank[5][:, 256 * a:256 * a + 256],
                                              ACT.Identity, bias=cc[:, a:a + 1], scale=1.0)
                    last.then_inc(tT_copied, 1)
                if at_group(it, c, 0):
                    act.wait_ge(layer1_paired, 1)
                    copy(Whi[:, 2, :], bank[1][:, 256:512], weights_copied)
                    act.activation(M1[:], bank[3][:, 256:512].rearrange("p (a n) -> p a n", a=2), ACT.Copy,
                                   scale=SCALE).then_inc(weights_copied, 1)
                if at_group(it, c, 1):
                    act.wait_ge(wr1_multiplied, 1)
                    act.activation(wr1[:], bank[1][:, 0:256], ACT.Copy, scale=SCALE).then_inc(weights_copied, 1)
                if live(it, c - 1):
                    act.wait_ge(ctxT_ready, upto(it, c - 1))
                    copy(chi[:], bank[3][:], chi_made)
                if live(it, c - 2):
                    act.wait_ge(oT_ready, upto(it, c - 2))
                    copy(ohi[:], bank[1][:], ohi_made)
                if live(it, c - 3):
                    act.wait_ge(nmax1_found, upto(it, c - 3))
                    for b in range(PER):
                        last = act.activation(prob1[:, b, :], bank[0][:, 128 * b:128 * b + 128], ACT.Exp,
                                              bias=nmax1[:, b:b + 1], scale=1.0, accum_out=rs1[:, b:b + 1])
                    last.then_inc(exp1_done, 1)
                if live(it, c):
                    act.wait_ge(max_found, upto(it, c))
                    for j in range(4):
                        last = act.activation(prob[:, j, :], bank[5][:, 128 * j:128 * j + 128], ACT.Exp,
                                              bias=nmax[:, j:j + 1], scale=1.0, accum_out=rs[:, j:j + 1])
                    last.then_inc(exp_done, 1)
                if at_group(it, c, 0):
                    act.wait_ge(W_centred, 1)
                    copy(Whi[:, 0:2, :], bank[0][:].rearrange("p (a n) -> p a n", a=2), weights_copied)
                if live(it, c - 3):
                    act.wait_ge(prob1T_ready, upto(it, c - 3))
                    copy(prob1T[:], bank[4][:, 0:256], prob1T_copied)
                if live(it, c):
                    act.wait_ge(sum_inverted, upto(it, c))
                    for j in range(4):
                        last = act.activation(prob[:, j, :], prob[:, j, :], ACT.Copy, scale=ri[:, j:j + 1])
                    last.then_inc(prob_normed, 1)

            run(act, iteration, start=0, last=LAST + 1)

        @block.tensor
        def _(pe):
            def split(dst, hi, lo, rhi, rlo, first, last):
                pe.matmul(dst, hi, rhi, start=first, stop=False)
                pe.matmul(dst, hi, rlo, start=False, stop=False)
                return pe.matmul(dst, lo, rhi, start=False, stop=last)

            def product(dst, lhsT, rhs):
                for e in range(CE):
                    last = pe.matmul(dst, lhsT(e), rhs(e), start=(e == 0), stop=(e == CE - 1))
                return last

            def x_turned(it, c):
                pe.wait_ge(x_normed, upto(it, c))
                wait(pe, o_added, upto(it, c - 2))
                for d in range(CQ):
                    for b in range(PER):
                        at = 256 * d + 128 * b
                        last = pe.transpose(bank[2][:, at:at + 128], xn[c % 2][:, b, 128 * d:128 * d + 128], ident[:])
                last.then_inc(xT_ready, 1)

            def yv_turned(it, c):
                pe.wait_ge(yv_normed, upto(it, c))
                for a in range(2):
                    for b in range(PER):
                        at = 256 * a + 128 * b
                        last = pe.transpose(bank[4][:, at:at + 128], yvn[c % 4][:, a, b, :], ident[:])
                last.then_inc(yvT_ready, 1)

            def queries(it, c):
                pe.wait_ge(x_split, upto(it, c))
                for a in range(2):
                    for d in range(CQ):
                        at = slice(256 * d, 256 * d + 256)
                        last = split(bank[5][:, 256 * a:256 * a + 256], Ahi[:, d, a, :], Alo[:, d, a, :],
                                     xhi[:, at], xlo[:, at], d == 0, d == CQ - 1)
                last.then_inc(t_ready, 1)

            def scores(it, c):
                pe.wait_ge(tT_copied, upto(it, c))
                pe.wait_ge(yvT_copied, upto(it, c))
                for j in range(4):
                    at = slice(128 * j, 128 * j + 128)
                    last = pe.matmul(bank[5][:, at], tT[:, at], yvT[:, at], start=True, stop=True)
                last.then_inc(s_ready, 1)

            def iteration(it, c):
                if live(it, c):
                    x_turned(it, c)
                if live(it, c):
                    yv_turned(it, c)
                if live(it, c - 3):
                    n = c - 3
                    pe.wait_ge(x1_added, upto(it, n))
                    for d in range(CQ):
                        for b in range(PER):
                            at = 256 * d + 128 * b
                            last = pe.transpose(bank[3][:, at:at + 128], X1[n % 2][:, b, 128 * d:128 * d + 128], ident[:])
                    last.then_inc(x1T_ready, 1)
                if at_group(it, c, 1):
                    pe.wait_ge(layer1_folded, 1)
                    pe.wait_ge(c_ready, 1)
                    product(bank[6][:, 256:512], lambda e: bvrep[:, e, :], lambda e: Wo[2][:, e, :])
                    product(bank[6][0:1, 0:256], lambda e: col[:, LNB + e:LNB + e + 1],
                            lambda e: fcW[:, e, :]).then_inc(offsets_multiplied, 1)
                if live(it, c - 1):
                    pe.wait_ge(prob_normed, upto(it, c - 1))
                    for j in range(4):
                        last = pe.transpose(bank[7][:, 128 * j:128 * j + 128], prob[:, j, :], ident[:])
                    last.then_inc(probT_ready, 1)
                if live(it, c - 4):
                    pe.wait_ge(c1_split, upto(it, c - 4))
                    wait(pe, final_added, upto(it, c - 5))
                    for b in range(PER):
                        at = slice(128 * b, 128 * b + 128)
                        last = split(bank[6][:, 256 * b:256 * b + 256], c1hi[:, at], c1lo[:, at],
                                     Whi[:, 2, :], Wlo[:, 2, :], True, True)
                    last.then_inc(proj1_ready, 1)
                if live(it, c):
                    queries(it, c)
                if at_group(it, c, 1):
                    pe.wait_ge(W1_ready, 1)
                    pe.wait_ge(weights_copied, 2)
                    product(bank[1][:, 0:256], lambda e: bkrep[:, e, :],
                            lambda e: WqT[2][:, e, :]).then_inc(wr1_multiplied, 1)
                if live(it, c - 3):
                    pe.wait_ge(x1_split, upto(it, c - 3))
                    if live(it, c - 1):
                        pe.wait_ge(probT_copied, upto(it, c - 1))
                    for d in range(CQ):
                        at = slice(256 * d, 256 * d + 256)
                        last = split(bank[7][:, 0:256], M1hi[:, d, :], M1lo[:, d, :], x1hi[:, at], x1lo[:, at],
                                     d == 0, d == CQ - 1)
                    last.then_inc(t1_ready, 1)
                if live(it, c - 1):
                    pe.wait_ge(probT_copied, upto(it, c - 1))
                    for a in range(2):
                        for b in range(PER):
                            at = slice(256 * a + 128 * b, 256 * a + 128 * b + 128)
                            last = pe.matmul(bank[3][:, at], yvn[(c - 1) % 4][:, a, b, :], probT[:, at], start=True, stop=True)
                    last.then_inc(ctxT_ready, 1)
                if live(it, c - 3):
                    n = c - 3
                    pe.wait_ge(y1_loaded[n % 4], nth(it, n, 4, 32))
                    pe.wait_ge(t1T_copied, upto(it, n))
                    for b in range(PER):
                        at = slice(128 * b, 128 * b + 128)
                        last = pe.matmul(bank[0][:, at], t1T[:, at], Y1T[n % 4][:, b, :], start=True, stop=True)
                    last.then_inc(s1_ready, 1)
                if live(it, c - 2):
                    pe.wait_ge(o_normed, upto(it, c - 2))
                    for d in range(CQ):
                        for b in range(PER):
                            at = 256 * d + 128 * b
                            last = pe.transpose(bank[1][:, at:at + 128], on[c % 2][:, b, 128 * d:128 * d + 128], ident[:])
                    last.then_inc(oT_ready, 1)
                if live(it, c):
                    scores(it, c)
                if live(it, c - 1):
                    pe.wait_ge(c_split, upto(it, c - 1))
                    if at_group(it, c, 1):
                        pe.wait_ge(weights_copied, 4)
                        pe.wait_ge(W_ready, 1)
                    for b in range(PER):
                        for a in range(2):
                            at = slice(256 * a + 128 * b, 256 * a + 128 * b + 128)
                            last = split(bank[2][:, 256 * b:256 * b + 256], chi[:, at], clo[:, at],
                                         Whi[:, a, :], Wlo[:, a, :], a == 0, a == 1)
                    last.then_inc(proj_ready, 1)
                if live(it, c - 3):
                    pe.wait_ge(exp1_done, upto(it, c - 3))
                    for b in range(PER):
                        last = pe.transpose(bank[4][:, 128 * b:128 * b + 128], prob1[:, b, :], ident[:])
                    last.then_inc(prob1T_ready, 1)
                if live(it, c - 2):
                    pe.wait_ge(o_split, upto(it, c - 2))
                    if at_group(it, c, 2):
                        pe.wait_ge(F_ready, 1)
                    for b in range(PER):
                        for d in range(CQ):
                            at = slice(256 * d + 128 * b, 256 * d + 128 * b + 128)
                            last = split(bank[0][:, 256 * b:256 * b + 256], ohi[:, at], olo[:, at],
                                         Fhi[:, d, :], Flo[:, d, :], d == 0, d == CQ - 1)
                    last.then_inc(fc_ready, 1)
                if live(it, c - 3):
                    n = c - 3
                    pe.wait_ge(prob1T_copied, upto(it, n))
                    for b in range(PER):
                        at = slice(128 * b, 128 * b + 128)
                        last = pe.matmul(bank[1][:, at], Y1[n % 4][:, b, :], prob1T[:, at], start=True, stop=True)
                    last.then_inc(ctx1T_ready, 1)

            pe.wait_ge(scores_w_loaded, 16 * 2)
            pe.wait_ge(kb_folded, 1)
            for a in range(2):
                for d in range(CQ):
                    last = product(bank[6 + a][:, 192 * d:192 * d + 129], lambda e: WqT[a][:, e, 128 * d:128 * d + 128],
                                   lambda e: WkT[a][:, e, :])
            last.then_inc(qk_multiplied, 1)
            pe.wait_ge(idents_made, 2)
            x_turned(0, 0)
            pe.wait_ge(values_w_loaded, 16 * 4)

            def values_product(a):
                product(bank[0][:, 256 * a:256 * a + 256], lambda e: WvT[a][:, e, :], lambda e: Wo[a][:, e, :])

            values_product(0)
            pe.wait_ge(A_ready, 1)
            yv_turned(0, 0)
            queries(0, 0)
            pe.wait_ge(qb_folded, 1)
            for a in range(2):
                last = product(bank[6][0:1, 192 * a:192 * a + 129], lambda e: qb[:, a, e:e + 1], lambda e: WkT[a][:, e, :])
            last.then_inc(qb_multiplied, 1)
            values_product(1)
            pe.wait_ge(crow_made, 1)
            for a in range(2):
                last = pe.matmul(bank[7][:, a:a + 1], crow[0:1, a, :], ones[0:1, 0:1], start=True, stop=True)
            last.then_inc(c_turned, 1)
            pe.wait_ge(vb_folded, 1)
            for a in range(2):
                last = product(bank[6][0:1, 256 * a:256 * a + 256], lambda e: vb[:, a, e:e + 1], lambda e: Wo[a][:, e, :])
            last.then_inc(vb_multiplied, 1)
            pe.wait_ge(layer1_w_loaded, 16 * 6)
            product(bank[1][:, 256:512], lambda e: WvT[2][:, e, :], lambda e: Wo[2][:, e, :])
            for d in range(CQ):
                last = product(bank[3][:, 256 + 128 * d:384 + 128 * d], lambda e: WqT[2][:, e, 128 * d:128 * d + 128],
                               lambda e: WkT[2][:, e, 0:DK])
            last.then_inc(layer1_paired, 1)
            scores(0, 0)
            pe.wait_ge(W_scaled, 1)
            for a in range(2):
                dst = bank[0][:, 256 * a:256 * a + 256]
                pe.matmul(dst, center[:], Wg[:, a, :], start=True, stop=False)
                last = pe.matmul(dst, ones[0:1, :], brow[0:1, a, :], start=False, stop=True)
            last.then_inc(W_centred, 1)

            iteration(0, 1)
            pe.wait_ge(F_scaled, 1)
            for k in range(CQ):
                pe.matmul(bank[0][:, 0:256], neg[:], Fg[:, k, :], start=(k == 0), stop=False)
            pe.matmul(bank[0][:, 0:256], ones[0:1, :], frow[0:1, 1, :], start=False, stop=True)
            product(bank[6][:, 0:1], lambda e: WkT[2][:, e, 0:DK], lambda e: qb1[:, e:e + 1])
            product(bank[6][:, 1:2], lambda e: bkrep[:, e, :], lambda e: qb1[:, e:e + 1]).then_inc(F_averaged, 1)
            run(pe, iteration, start=2, last=LAST + 1)

        @block.vector
        def _(dve):
            def on_rows(t, n, length):
                return t[:, 0:n].unsqueeze(2).broadcast_to([128, n, length])

            def lo_part(dst, src, hi, s):
                dve.tensor_tensor(dst[:], src, hi[:].bitcast(F32), ALU.subtract).then_inc(s, 1)

            def x_stats(it, n):
                dve.wait_ge(x_loaded[n % 4], nth(it, n, 4))
                for b in range(PER):
                    last = dve.bn_stats(inst[n % 2][:, b, :], X[n % 4][:, b, :])
                last.then_inc(in_stats, 1)

            def yv_stats(it, n):
                wait(dve, yv_normed, upto(it, n - 2))
                dve.wait_ge(yv_loaded[n % 4], nth(it, n, 4, 32))
                for a in range(2):
                    for b in range(PER):
                        dve.bn_stats(inst[n % 2][:, PER + PER * a + b, :], YV[n % 4][:, a, b, :])

            def x_rest(it, c):
                dve.wait_ge(xhi_made, upto(it, c))
                lo_part(xlo, bank[2][:], xhi, x_split)

            def largest(it, c):
                dve.wait_ge(s_ready, upto(it, c))
                dve.tensor_reduce(nmax[:], bank[5][:].rearrange("p (j k) -> p j k", j=4), AX.X, ALU.max,
                                  negate=True).then_inc(max_found, 1)

            def result(it, c):
                n = c - 4
                dve.wait_ge(proj1_ready, upto(it, n))
                dve.wait_ge(sum1_inverted, upto(it, n))
                wait(dve, stored[n % 2], nth(it, n - 2, 2))
                for b in range(PER):
                    last = dve.scalar_tensor_tensor(out=fin[n % 2][:, b, :], in0=bank[6][:, 256 * b:256 * b + 256],
                                                    scalar=ri1[:, b:b + 1], in1=X1[n % 2][:, b, :],
                                                    op0=ALU.mult, op1=ALU.add)
                last.then_inc(final_added, 1)

            def inverted(it, c):
                dve.wait_ge(exp_done, upto(it, c))
                dve.reciprocal(ri[:], rs[:]).then_inc(sum_inverted, 1)

            def row_sums(k, mat, vector, begin, dst, scale=1.0):
                return dve.tensor_tensor_reduce(scratch[:, k, 0:vector.shape[-1]], mat, vector, scale, begin,
                                                ALU.mult, ALU.add, dst)

            def halves(t):
                return t.rearrange("p (a n) -> p a n", a=2)

            def iteration(it, c):
                if live(it, c - 4):
                    dve.wait_ge(c1hi_made, upto(it, c - 4))
                    lo_part(c1lo, bank[1][:, 0:256], c1hi, c1_split)
                if at_group(it, c, 1):
                    dve.wait_ge(weights_copied, 3)
                    dve.tensor_tensor(Wlo[:, 0:2, :], halves(bank[0][:]), Whi[:, 0:2, :].bitcast(F32),
                                      ALU.subtract).then_inc(W_ready, 1)
                if live(it, c):
                    x_rest(it, c)
                if at_group(it, c, 1):
                    dve.tensor_copy(M1hi[:], M1[:]).then_inc(weights_step, 1)
                    for d in range(CQ):
                        dve.tensor_scalar(Fg[:, d, :], fcW[:, d, :], col[:, LNG + d:LNG + d + 1], None, ALU.mult)
                    dve.wait_ge(offsets_multiplied, 1)
                    dve.tensor_tensor(bias1[:], bank[6][:, 256:512], wide[:, BO1_AT:BO1_AT + DQ], ALU.add).then_inc(weights_step, 1)
                    dve.tensor_tensor(frow[0:1, 0, :], bank[6][0:1, 0:256], row[0:1, 2, :], ALU.add).then_inc(weights_step, 1)
                    dve.wait_ge(weights_step, 21)
                    dve.tensor_tensor(M1lo[:], M1[:], M1hi[:].bitcast(F32), ALU.subtract)
                    dve.tensor_tensor(frow[0:1, 1, :], frow[0:1, 0, :], bias1[0:1, :], ALU.add)
                    for e in range(CE):
                        last = row_sums(12 + e, WqT[2][:, e, :], bias1[:], col[:, BQ + 4 + e:BQ + 5 + e], qb1[:, e:e + 1], -1.0)
                    last.then_inc(F_scaled, 1)
                if at_group(it, c, 2):
                    dve.wait_ge(F_averaged, 1)
                    dve.tensor_scalar(cc[:, 2:4], bank[6][:, 0:2], SCALE, None, ALU.mult)
                    for d in range(CQ):
                        dve.tensor_tensor(Ff[:, d, :], Fg[:, d, :], bank[0][:, 0:256], ALU.add).then_inc(weights_step, 1)
                    dve.wait_ge(weights_step, 23)
                    dve.tensor_copy(Fhi[:], Ff[:]).then_inc(weights_step, 1)
                    dve.wait_ge(weights_step, 24)
                    dve.tensor_tensor(Flo[:], Ff[:], Fhi[:].bitcast(F32), ALU.subtract).then_inc(F_ready, 1)
                if live(it, c - 3):
                    dve.wait_ge(x1hi_made, upto(it, c - 3))
                    lo_part(x1lo, bank[3][:], x1hi, x1_split)
                if live(it, c - 4):
                    result(it, c)
                if live(it, c - 3):
                    n = c - 3
                    dve.wait_ge(x1_added, upto(it, n))
                    for b in range(PER):
                        last = dve.tensor_tensor_reduce(junk[:, b, :], X1[n % 2][:, b, :], wr1[:], 1.0, cc[:, 3:4],
                                                        ALU.mult, ALU.add, r1[n % 2][:, b:b + 1])
                    last.then_inc(r1_found, 1)
                if live(it, c + 2):
                    yv_stats(it, c + 2)
                if live(it, c + 2):
                    x_stats(it, c + 2)
                if live(it, c - 3):
                    dve.wait_ge(s1_ready, upto(it, c - 3))
                    dve.tensor_reduce(max1[:], bank[0][:, 0:256].rearrange("p (b k) -> p b k", b=PER), AX.X,
                                      ALU.max).then_inc(max1_found, 1)
                if live(it, c - 1):
                    dve.wait_ge(chi_made, upto(it, c - 1))
                    lo_part(clo, bank[3][:], chi, c_split)
                if live(it, c - 3):
                    n = c - 3
                    dve.wait_ge(max1_found, upto(it, n))
                    dve.wait_ge(r1_found, upto(it, n))
                    dve.tensor_tensor(top1[:], max1[:], r1[n % 2][:], ALU.add).then_inc(top1_found, 1)
                    dve.wait_ge(top1_found, upto(it, n))
                    dve.tensor_tensor(nmax1[:], r1[n % 2][:], top1[:], ALU.subtract).then_inc(nmax1_found, 1)
                if live(it, c):
                    largest(it, c)
                if live(it, c - 2):
                    dve.wait_ge(ohi_made, upto(it, c - 2))
                    lo_part(olo, bank[1][:], ohi, o_split)
                if live(it, c - 3):
                    dve.wait_ge(exp1_done, upto(it, c - 3))
                    if live(it, c - 4):
                        dve.wait_ge(final_added, upto(it, c - 4))
                    dve.reciprocal(ri1[:], rs1[:]).then_inc(sum1_inverted, 1)
                if live(it, c - 1):
                    n = c - 1
                    dve.wait_ge(proj_ready, upto(it, n))
                    dve.tensor_tensor(O[n % 2][:], halves(bank[2][:]), X[n % 4][:], ALU.add).then_inc(o_added, 1)
                if live(it, c):
                    inverted(it, c)
                if live(it, c - 1):
                    n = c - 1
                    dve.wait_ge(o_added, upto(it, n))
                    for b in range(PER):
                        last = dve.bn_stats(outst[n % 2][:, b, :], O[n % 2][:, b, :])
                    last.then_inc(out_stats, 1)
                if live(it, c - 1):
                    dve.wait_ge(out_stats, upto(it, c - 1))
                if live(it, c - 2):
                    n = c - 2
                    dve.wait_ge(fc_ready, upto(it, n))
                    dve.tensor_tensor(X1[n % 2][:], halves(bank[0][:]), O[n % 2][:], ALU.add).then_inc(x1_added, 1)
                if live(it, c - 1):
                    n = c - 1
                    for b in range(PER):
                        last = dve.bn_aggr(outmv[n % 2][:, b, :], outst[n % 2][:, b, :])
                    last.then_inc(out_aggregated, 1)

            yv_stats(0, 0)
            x_stats(0, 0)
            dve.wait_ge(keys_w_loaded, 16 * 4)
            for k in range(4):
                a, e = k // 2, k % 2
                last = row_sums(k, WkT[a][:, e, 0:DK], b2(a), col[:, BK + k:BK + k + 1], WkT[a][:, e, DK:DK + 1])
            last.then_inc(kb_folded, 1)
            dve.tensor_scalar(g1s[:], col[:, G1:G1 + 4], SCALE, None, ALU.mult).then_inc(weights_step, 1)
            dve.wait_ge(qk_multiplied, 1)
            for k in range(4):
                a, d = k // 2, k % 2
                dve.tensor_tensor_reduce(U[:, k, :], bank[6 + a][:, 192 * d:192 * d + 128], g2(a), 1.0, 0.0,
                                         ALU.mult, ALU.add, usum[:, k:k + 1]).then_inc(weights_step, 1)
            dve.wait_ge(weights_step, 5)
            for k in range(4):
                a, d = k // 2, k % 2
                dve.scalar_tensor_tensor(out=usc[:, k:k + 1], in0=usum[:, k:k + 1], scalar=-1.0 / DK,
                                         in1=bank[6 + a][:, 192 * d + 128:192 * d + 129],
                                         op0=ALU.mult, op1=ALU.add).then_inc(weights_step, 1)
            dve.wait_ge(weights_step, 9)
            for k in range(4):
                a, d = k // 2, k % 2
                dve.tensor_scalar(Af[:, d, a, :], U[:, k, :], usc[:, k:k + 1], g1s[:, k:k + 1],
                                  ALU.add, ALU.mult).then_inc(weights_step, 1)
            dve.wait_ge(weights_step, 13)
            dve.tensor_copy(Ahi[:], Af[:]).then_inc(weights_step, 1)
            dve.wait_ge(weights_step, 14)
            dve.tensor_tensor(Alo[:], Af[:], Ahi[:].bitcast(F32), ALU.subtract).then_inc(A_ready, 1)
            x_rest(0, 0)
            dve.wait_ge(q_vectors_loaded, 16)
            dve.wait_ge(scores_w_loaded, 16 * 2)
            for k in range(4):
                a, e = k // 2, k % 2
                last = row_sums(4 + k, WqT[a][:, e, :], b1(a), col[:, BQ + k:BQ + k + 1], qb[:, a, e:e + 1])
            last.then_inc(qb_folded, 1)
            yv_stats(0, 1)
            x_stats(0, 1)
            dve.wait_ge(qb_multiplied, 1)
            for a in range(2):
                dve.tensor_tensor_reduce(Urow[0:1, a, :], bank[6][0:1, 192 * a:192 * a + 128], g2(a, 1), 1.0, 0.0,
                                         ALU.mult, ALU.add, usum[0:1, 4 + a:5 + a]).then_inc(weights_step, 1)
            dve.wait_ge(weights_step, 16)
            for a in range(2):
                dve.scalar_tensor_tensor(out=usc[0:1, 4 + a:5 + a], in0=usum[0:1, 4 + a:5 + a], scalar=-1.0 / DK,
                                         in1=bank[6][0:1, 192 * a + 128:192 * a + 129],
                                         op0=ALU.mult, op1=ALU.add).then_inc(weights_step, 1)
            dve.wait_ge(weights_step, 18)
            for a in range(2):
                last = dve.tensor_scalar(crow[0:1, a, :], Urow[0:1, a, :], usc[0:1, 4 + a:5 + a], SCALE,
                                         ALU.add, ALU.mult)
            last.then_inc(crow_made, 1)
            dve.wait_ge(values_w_loaded, 16 * 4)
            for k in range(4):
                a, e = k // 2, k % 2
                last = row_sums(8 + k, WvT[a][:, e, :], b2(a), col[:, BV + k:BV + k + 1], vb[:, a, e:e + 1])
            last.then_inc(vb_folded, 1)
            dve.wait_ge(c_turned, 1)
            dve.tensor_copy(cc[:, 0:2], bank[7][:, 0:2]).then_inc(c_ready, 1)
            dve.tensor_copy(bkrep[:], on_rows(col[:, BK + 4:BK + 6], CE, 128))
            dve.tensor_copy(bvrep[:], on_rows(col[:, BV + 4:BV + 6], CE, 128)).then_inc(layer1_folded, 1)
            dve.wait_ge(vb_multiplied, 1)
            dve.wait_ge(layer1_w_loaded, 16 * 6)
            for a in range(2):
                dve.tensor_tensor(brow[0:1, a, :], bank[6][0:1, 256 * a:256 * a + 256], row[0:1, a, :], ALU.add)
                last = dve.tensor_scalar(Wg[:, a, :], bank[0][:, 256 * a:256 * a + 256], col[:, G2 + a:G2 + a + 1], None,
                                         ALU.mult)
            last.then_inc(W_scaled, 1)
            dve.wait_ge(weights_copied, 1)
            dve.tensor_tensor(Wlo[:, 2, :], bank[1][:, 256:512], Whi[:, 2, :].bitcast(F32),
                              ALU.subtract).then_inc(W1_ready, 1)
            largest(0, 0)
            yv_stats(0, 2)
            x_stats(0, 2)
            inverted(0, 0)
            run(dve, iteration, start=1, last=LAST + 1)


def kernel(**inputs):
    import numpy as _np
    import concourse.bacc as _bacc
    from concourse import mybir as _mybir
    from concourse.bass_utils import run_bass_kernel_spmd as _run

    def get(name):
        return _np.ascontiguousarray(inputs[name])

    def columns(name):
        return get(name).reshape(-1, 128).T

    def layout(a):
        return _np.ascontiguousarray(a)

    la, lv, l1 = "L0_xattn_a_", "L0_xattn_v_", "L1_xattn_"
    arrays = {"x": get("x"), "ctx": get("ctx_512"), "ctxT": layout(get("ctx_512").transpose(0, 2, 1)),
              "fside": get("fside_BxSxS_0")}
    for a, p in enumerate((la, lv, l1)):
        arrays[f"WqT{a}"] = layout(get(p + "Wq").T)
        arrays[f"WkT{a}"] = layout(get(p + "Wk").T)
        arrays[f"WvT{a}"] = layout(get(p + "Wv").T)
        arrays[f"Wo{a}"] = get(p + "Wo")
    arrays["fcW"] = get("L0_xattn_fc_W")
    arrays["cols"] = layout(_np.concatenate([columns(n) for n in (
        la + "bk", lv + "bk", l1 + "bk", la + "bq", lv + "bq", l1 + "bq", la + "bv", lv + "bv", l1 + "bv",
        la + "ln1_g", lv + "ln1_g", la + "ln2_g", lv + "ln2_g", "L0_xattn_ln_g", "L0_xattn_ln_b")], axis=1))
    arrays["rows"] = layout(_np.stack([get(la + "bo"), get(lv + "bo"), get("L0_xattn_fc_b")])[None])
    arrays["wide_rows"] = layout(_np.concatenate([get(n) for n in (
        la + "ln2_b", lv + "ln2_b", la + "ln2_g", lv + "ln2_g", la + "ln1_b", lv + "ln1_b", l1 + "bo")]))

    nc = _bacc.Bacc("TRN2", target_bir_lowering=False, num_devices=1)
    aps = {name: nc.dram_tensor(f"in_{name}", a.shape, _mybir.dt.from_np(a.dtype), kind="ExternalInput").ap()
           for name, a in arrays.items()}
    out = nc.dram_tensor("out_0", (BATCH, SEQ, DQ), F32, kind="ExternalOutput").ap()
    build(nc, aps["x"], aps["ctx"], aps["ctxT"], aps["fside"], aps, aps["cols"], aps["rows"], aps["wide_rows"], out)
    r = _run(nc, [{f"in_{name}": a for name, a in arrays.items()}], core_ids=[0])
    return r.results[0]["out_0"]
```
